# Optimizing a Trainium2 kernel written in Bass

```python
import numpy as np
import jax
import jax.numpy as jnp

def _softmax(x, axis=-1):
    return jax.nn.softmax(x, axis=axis)

def _gelu(x):
    return jax.nn.gelu(x, approximate=True)

def _silu(x):
    return jax.nn.silu(x)

def _sigmoid(x):
    return jax.nn.sigmoid(x)

def _layernorm(x, axis=-1, eps=1e-05):
    m = jnp.mean(x, axis=axis, keepdims=True)
    v = jnp.var(x, axis=axis, keepdims=True)
    return (x - m) / jnp.sqrt(v + eps)

def _scatter_add(tgt, idx, src, axis=0):
    return tgt.at[idx].add(src)

def _segment_sum(src, seg, n):
    return jax.ops.segment_sum(src, seg, n)
kernel_name = 'mk_conv_attn_hybrid_d2_conv_nchw256_r4_57004c'

def setup_inputs(seed: int=0):
    np.random.seed(seed)
    _w = jnp.asarray

    def _rec_inputs():
        import jax
        import jax.numpy as jnp
        _gk = jax.random.key(seed)
        x = -0.0002023 + 1 * jax.random.normal(jax.random.fold_in(_gk, 1), (8, 64, 56, 56), jnp.float32)
        return x
    x = _rec_inputs()

    def _L0_conv_setup():
        import jax, jax.numpy as jnp
        import numpy as np
        KH, KW = (3, 3)
        PAD = 1
        STRIDE = 1
        IN_CH, OUT_CH = (64, 64)
        SPARSITY = 0.9
        key = jax.random.key(seed)
        kx, kw, km = jax.random.split(key, 3)
        x = jax.random.normal(kx, (8, IN_CH, 56, 56), dtype=jnp.float32)
        in_feats = IN_CH * KH * KW
        w_dense = jax.random.normal(kw, (OUT_CH, in_feats), dtype=jnp.float32) * 0.05
        mask = (jax.random.uniform(km, (OUT_CH, in_feats)) > SPARSITY).astype(jnp.float32)
        weight = w_dense * mask
        return {'x': x, 'weight': weight}
    _L0_conv_all = _L0_conv_setup()
    _L0_conv_in = {k: v for k, v in _L0_conv_all.items() if k in ('weight',)}
    del _L0_conv_all

    def _L1_attn_setup():
        import jax, jax.numpy as jnp
        import numpy as np
        B, S, D = (4, 1024, 64)
        key = jax.random.key(seed)
        ks = jax.random.split(key, 7)
        s = 1.0 / np.sqrt(D)
        return {'x': jax.random.normal(ks[0], (B, S, D), dtype=jnp.float32), 'Wq': jax.random.normal(ks[1], (D, D), dtype=jnp.float32) * s, 'bq': jax.random.normal(ks[2], (D,), dtype=jnp.float32) * s, 'Wk': jax.random.normal(ks[3], (D, D), dtype=jnp.float32) * s, 'bk': jax.random.normal(ks[4], (D,), dtype=jnp.float32) * s, 'Wv': jax.random.normal(ks[5], (D, D), dtype=jnp.float32) * s, 'bv': jax.random.normal(ks[6], (D,), dtype=jnp.float32) * s}
    _L1_attn_all = _L1_attn_setup()
    _L1_attn_in = {k: v for k, v in _L1_attn_all.items() if k in ('Wq', 'bq', 'Wk', 'bk', 'Wv', 'bv')}
    del _L1_attn_all

    def _L1_ffn_setup():
        import jax, jax.numpy as jnp
        import numpy as np
        D_MODEL = 64
        N_EXPERTS = 16
        HIDDEN = 128
        SCALE = 0.02
        key = jax.random.key(seed)
        ks = jax.random.split(key, 5)
        x = jax.random.normal(ks[0], (4, 2048, D_MODEL), dtype=jnp.float32)
        gate_w = jax.random.normal(ks[1], (D_MODEL, N_EXPERTS), dtype=jnp.float32) * SCALE
        gate_b = jnp.zeros((N_EXPERTS,), dtype=jnp.float32)
        w1 = jax.random.normal(ks[2], (N_EXPERTS, D_MODEL, HIDDEN), dtype=jnp.float32) * SCALE
        w2 = jax.random.normal(ks[3], (N_EXPERTS, D_MODEL, HIDDEN), dtype=jnp.float32) * SCALE
        w3 = jax.random.normal(ks[4], (N_EXPERTS, HIDDEN, D_MODEL), dtype=jnp.float32) * SCALE
        return {'x': x, 'gate_w': gate_w, 'gate_b': gate_b, 'w1': w1, 'w2': w2, 'w3': w3}
    _L1_ffn_all = _L1_ffn_setup()
    _L1_ffn_in = {k: v for k, v in _L1_ffn_all.items() if k in ('gate_w', 'gate_b', 'w1', 'w2', 'w3')}
    del _L1_ffn_all
    return {'x': x, 'L0_conv_weight': _L0_conv_in['weight'], 'L1_attn_Wq': _L1_attn_in['Wq'], 'L1_attn_bq': _L1_attn_in['bq'], 'L1_attn_Wk': _L1_attn_in['Wk'], 'L1_attn_bk': _L1_attn_in['bk'], 'L1_attn_Wv': _L1_attn_in['Wv'], 'L1_attn_bv': _L1_attn_in['bv'], 'L1_ffn_gate_w': _L1_ffn_in['gate_w'], 'L1_ffn_gate_b': _L1_ffn_in['gate_b'], 'L1_ffn_w1': _L1_ffn_in['w1'], 'L1_ffn_w2': _L1_ffn_in['w2'], 'L1_ffn_w3': _L1_ffn_in['w3']}

def reference(x, L0_conv_weight, L1_attn_Wq, L1_attn_bq, L1_attn_Wk, L1_attn_bk, L1_attn_Wv, L1_attn_bv, L1_ffn_gate_w, L1_ffn_gate_b, L1_ffn_w1, L1_ffn_w2, L1_ffn_w3):
    import jax
    import jax.numpy as jnp

    def _L0_conv_ref(x, weight):
        import jax, jax.numpy as jnp
        import numpy as np
        KH, KW = (3, 3)
        PAD = 1
        STRIDE = 1
        IN_CH, OUT_CH = (64, 64)
        SPARSITY = 0.9
        patches = jax.lax.conv_general_dilated_patches(x, filter_shape=(KH, KW), window_strides=(STRIDE, STRIDE), padding=((PAD, PAD), (PAD, PAD)))
        B, F, Ho, Wo = patches.shape
        out = jnp.einsum('of,bfp->bop', weight, patches.reshape(B, F, Ho * Wo))
        return out.reshape(B, weight.shape[0], Ho, Wo)

    def _L1_attn_ref(x, Wq, bq, Wk, bk, Wv, bv):
        import jax, jax.numpy as jnp
        import numpy as np
        B, S, D = (4, 1024, 64)
        q = jnp.einsum('bsd,ed->bse', x, Wq) + bq
        k = jnp.einsum('bsd,ed->bse', x, Wk) + bk
        v = jnp.einsum('bsd,ed->bse', x, Wv) + bv
        scale = 1.0 / jnp.sqrt(jnp.float32(x.shape[-1]))
        scores = jnp.einsum('bqd,bkd->bqk', q, k) * scale
        attn = jax.nn.softmax(scores, axis=-1)
        return jnp.einsum('bqk,bkd->bqd', attn, v)

    def _L1_ffn_ref(x, gate_w, gate_b, w1, w2, w3):
        import jax, jax.numpy as jnp
        import numpy as np
        D_MODEL = 64
        N_EXPERTS = 16
        HIDDEN = 128
        SCALE = 0.02
        n_experts = w1.shape[0]
        logits = jnp.einsum('bsd,de->bse', x, gate_w) + gate_b
        probs = jax.nn.softmax(logits, axis=-1)
        top_probs, top_idx = jax.lax.top_k(probs, 2)
        top_probs = top_probs / jnp.sum(top_probs, axis=-1, keepdims=True)
        dispatch = jnp.sum(jax.nn.one_hot(top_idx, n_experts, dtype=x.dtype) * top_probs[..., None], axis=-2)
        h1 = jnp.einsum('bsd,edh->bseh', x, w1)
        h2 = jnp.einsum('bsd,edh->bseh', x, w2)
        hidden = jax.nn.silu(h1) * h2
        expert_out = jnp.einsum('bseh,eho->bseo', hidden, w3)
        return jnp.einsum('bseo,bse->bso', expert_out, dispatch)

    def _gn(v, G=32, eps=1e-05):
        B_, C_, H_, W_ = v.shape
        g = v.reshape(B_, G, C_ // G, H_, W_)
        m = jnp.mean(g, axis=(2, 3, 4), keepdims=True)
        s = jnp.var(g, axis=(2, 3, 4), keepdims=True)
        return ((g - m) / jnp.sqrt(s + eps)).reshape(v.shape)

    def _ln_c(v, eps=1e-06):
        m = jnp.mean(v, axis=1, keepdims=True)
        s = jnp.var(v, axis=1, keepdims=True)
        return (v - m) / jnp.sqrt(s + eps)

    def _ln_t(v, eps=1e-05):
        m = jnp.mean(v, axis=-1, keepdims=True)
        s = jnp.var(v, axis=-1, keepdims=True)
        return (v - m) / jnp.sqrt(s + eps)

    def _to_tokens(v):
        B_, C_, H_, W_ = v.shape
        return v.reshape(B_, C_, H_ * W_).transpose(0, 2, 1)

    def _from_tokens(t, like):
        B_, C_, H_, W_ = like.shape
        return t.transpose(0, 2, 1).reshape(B_, C_, H_, W_)
    x = x + _L0_conv_ref(_gn(x), L0_conv_weight)
    t = _to_tokens(x)
    t = t + _L1_attn_ref(_ln_t(t), L1_attn_Wq, L1_attn_bq, L1_attn_Wk, L1_attn_bk, L1_attn_Wv, L1_attn_bv)
    t = t + _L1_ffn_ref(_ln_t(t), L1_ffn_gate_w, L1_ffn_gate_b, L1_ffn_w1, L1_ffn_w2, L1_ffn_w3)
    x = _from_tokens(t, x)
    return x

_drawn_inputs = setup_inputs


def setup_inputs(seed=0):
    import zlib

    import numpy as np

    out = dict(_drawn_inputs(seed))
    spreads = {'L1_ffn_gate_b': (0.0, 0.8)}
    factors = {'L1_attn_bq': 3.664,
     'L1_attn_bk': 8.0,
     'L1_ffn_gate_w': 8.0,
     'L1_ffn_w1': 8.0,
     'L1_ffn_w2': 8.0,
     'L1_ffn_w3': 8.0}
    for name, (base, spread) in spreads.items():
        noise = np.random.default_rng([zlib.crc32(name.encode()), seed]).standard_normal(out[name].shape)
        drawn = base * np.exp(spread * noise) if base else spread * noise
        out[name] = jnp.asarray(drawn.astype(out[name].dtype))
    for name, factor in factors.items():
        out[name] = (out[name] * factor).astype(out[name].dtype)
    return out
```

```python
import concourse.bass as bass
from concourse import mybir
from contextlib import ExitStack

f32 = mybir.dt.float32
f32r = mybir.dt.float32r
i32 = mybir.dt.int32
u32 = mybir.dt.uint32
ALU = mybir.AluOpType
ACT = mybir.ActivationFunctionType
AX = mybir.AxisListType

BATCHES, CHANNELS, SIDE = 8, 64, 56
TOKENS = SIDE * SIDE
ROWS = 8
CHUNK = ROWS * SIDE
CHUNKS = TOKENS // CHUNK
ALL = BATCHES * CHUNKS
TILE = 112
PER = CHUNK // TILE
TILES = TOKENS // TILE
PAD = SIDE + 2
TAPS = 9
EXPERTS, HIDDEN, TOP = 16, 128, 2
SLOTS = 128
SORTED_MOST = TOP * TOKENS // SLOTS + EXPERTS - 1
SLICE = -(-SORTED_MOST // CHUNKS)
PAIRS = SLICE // 2
SORTED_TILES = SLICE * CHUNKS
VCOLS = CHANNELS + 1
GN_EPS, LN_EPS = 1e-5, 1e-5
ONE = 1
ZEROS = 16 * CHUNKS
assert SLICE % 2 == 0 and TOKENS % CHUNK == 0

LAG = {"pre": -CHUNKS, "post": 1, "scatter": 1 + CHUNKS, "experts": 1 + 2 * CHUNKS, "combine": 1 + 3 * CHUNKS}
STEPS = [(0, "scatter", "scatter"), (0, "pre", "normed"), (1, "post", "attended"), (2, "pre", "conv"),
         (2, "held", "hold"), (3, "pre", "tokens"), (4, "pre", "norm1"), (5, "pre", "turned"), (6, "pre", "query"), (7, "pre", "key"),
         (7, "combine", "gather"), (7, "scatter", "rows"), (8, "post", "norm2"), (9, "post", "turned2"), (10, "post", "gate"),
         (15, "combine", "combine"), (18, "stats", "stats")]
EXPERT_STEPS = [(1 + 5 * g, "fx", g) for g in range(PAIRS)] + [(2 + 5 * g, "hidden", g) for g in range(PAIRS)] + \
               [(4 + 5 * g, "turn", g) for g in range(PAIRS)] + [(6 + 5 * g, "down", g) for g in range(PAIRS)]
EXPERT_STEPS.sort(key=lambda x: (x[0], {"down": 0, "fx": 1, "hidden": 2, "turn": 3}[x[1]]))
NEXT_QUERIES = 9
MAX_FROM, MAX_TO = 11, 26


def wait_apart(engine, sem, value):
    engine.wait_ge(sem, value)
    engine.nop(nofuse=True)


class Link:

    def __init__(self, engine, sem, start):
        self.engine, self.sem, self.start, self.count = engine, sem, start, 0

    def __call__(self, instruction, apart=False):
        instruction.then_inc(self.sem, 1)
        self.count += 1
        (wait_apart if apart else type(self.engine).wait_ge)(self.engine, self.sem, ONE + self.start + self.count)


class At:

    def __init__(self, u, c):
        self.u, self.c, self.static = u, c, isinstance(c, int)
        self.n = CHUNKS * u + c
        self.attends = 0 <= u < BATCHES
        self.ahead = self.attends and not (u == BATCHES - 1 and self.static and c == CHUNKS - 1)
        self.next_u = u + 1 if self.static and c == CHUNKS - 1 else u
        self.next_c = 0 if self.static and c == CHUNKS - 1 else c + 1

    def index(self, stage):
        first = CHUNKS * self.u - LAG[stage] + (self.c if self.static else 1)
        last = first if self.static else first + CHUNKS - 3
        if last < 0:
            return 0
        if first >= ALL:
            return ALL
        return CHUNKS * self.u - LAG[stage] + self.c

    def active(self, stage):
        if stage == "held":
            return self.attends
        if stage == "stats":
            return 0 <= self.u + 2 < BATCHES
        first = CHUNKS * self.u - LAG[stage] + (self.c if self.static else 1)
        return 0 <= first < ALL

    def batch(self, stage):
        return (CHUNKS * self.u - LAG[stage] + (self.c if self.static else 1)) // CHUNKS

    def chunk(self, stage):
        return self.index(stage) - CHUNKS * self.batch(stage)


def iterations(engine, body):
    for u in range(-2, BATCHES + 4):
        if u < BATCHES + 3:
            body(At(u, 0))
            with engine.Fori(1, CHUNKS - 1) as c:
                body(At(u, c))
            body(At(u, CHUNKS - 1))
        else:
            body(At(u, 0))


def build(nc, x, conv_w, wq, bq, wk, bk, wv, bv, gate_w, gate_b, w1, w2, w3, out):
    def scratch(name, shape):
        return nc.dram_tensor(name, shape, f32, kind="Internal").ap()

    sorted_x = [scratch(f"sorted_x{p}", (SORTED_TILES * SLOTS, CHANNELS)) for p in range(2)]
    sorted_y = [scratch(f"sorted_y{p}", (SORTED_TILES * SLOTS, CHANNELS)) for p in range(2)]
    kept = scratch("kept", (ALL, TILE, PER * CHANNELS))
    x_v = x.rearrange("b c h w -> b c (h w)")
    out_v = out.rearrange("b c h w -> b c (h w)")

    ctx = ExitStack()
    with ctx:
        def sb(name, shape, dt=f32):
            return ctx.enter_context(nc.sbuf_tensor(name, shape, dt))

        def pb(name, shape, dt=f32):
            return ctx.enter_context(nc.psum_tensor(name, shape, dt))

        ident = sb("ident", [128, 128])
        pair_mean = sb("pair_mean", [128, 128])
        before = sb("before", [TILE, TILE])
        ones = sb("ones", [TILE, TILE])
        minus_half = sb("minus_half", [128, PER])
        expert_i = sb("expert_i", [TILE, EXPERTS], i32)
        expert_f = sb("expert_f", [TILE, EXPERTS])
        tile_i = sb("tile_i", [TILE, SORTED_TILES], i32)
        tile_f = sb("tile_f", [TILE, SORTED_TILES])
        not_first = sb("not_first", [TILE, EXPERTS * TILES])
        raw_w = sb("raw_w", [128, (TAPS + 3) * CHANNELS])
        wT = sb("wT", [128, TAPS + 2, 128], f32r)
        w_out = sb("w_out", [VCOLS, VCOLS])
        w12 = sb("w12", [128, EXPERTS, 2 * HIDDEN], f32r)
        w3s = sb("w3s", [HIDDEN, EXPERTS, CHANNELS])
        gate_s = sb("gate_s", [CHANNELS, EXPERTS])
        gate_bb = sb("gate_bb", [TILE, EXPERTS])
        bq_raw = sb("bq_raw", [128, 1])
        bq_s = sb("bq_s", [128, 1])
        bk_s = sb("bk_s", [128, 1])

        x_st = sb("x_st", [128, CHUNK])
        gn_stats = sb("gn_stats", [128, CHUNKS, 6])
        gn_mv = sb("gn_mv", [128, 2])
        gn_mean, gn_d, gn_q, gn_e, gn_var, gn_rstd, gn_bias = [
            sb(f"gn_{n}", [128, 1]) for n in ("mean", "d", "q", "e", "var", "rstd", "bias")]
        xh = sb("xh", [128, ROWS + 2, SIDE])
        xg_f = sb("xg_f", [128, ROWS + 2, SIDE])
        xg_hi = sb("xg_hi", [128, ROWS + 2, PAD], f32r)
        xg_lo = sb("xg_lo", [128, ROWS + 2, PAD], f32r)
        x_conv = sb("x_conv", [CHANNELS, CHUNK])

        tok = sb("tok", [TILE, TILES, CHANNELS])
        tok_held = sb("tok_held", [TILE, PER, CHANNELS])
        ln_s = sb("ln_s", [TILE, 4, PER])
        ln_c = sb("ln_c", [TILE, PER, CHANNELS])
        ln_q = sb("ln_q", [TILE, PER, CHANNELS])
        xn = sb("xn", [TILE, PER, 2, CHANNELS])
        xn_hi = sb("xn_hi", [128, CHUNK], f32r)
        xn_lo = sb("xn_lo", [128, CHUNK], f32r)
        qk_f = sb("qk_f", [128, 2, CHUNK])
        qk_hi = sb("qk_hi", [128, CHUNK], f32r)
        q_hl = sb("q_hl", [128, TOKENS], f32r)
        k_a = [sb(f"k_a{p}", [128, TOKENS], f32r) for p in range(2)]
        k_b = [sb(f"k_b{p}", [128, TOKENS], f32r) for p in range(2)]
        v_s = [sb(f"v_s{p}", [TILE, TILES, VCOLS]) for p in range(2)]
        q_a = sb("q_a", [128, 2, CHUNK], f32r)
        q_b = sb("q_b", [128, 2, CHUNK], f32r)
        q_max = sb("q_max", [128, CHUNK], f32r)
        prob = [sb(f"prob{i}", [TILE, CHUNK]) for i in range(4)]
        max_part = sb("max_part", [TILE, PER, CHUNKS])
        max_neg = sb("max_neg", [TILE, PER])
        z_s = sb("z_s", [VCOLS, CHUNK])
        row_inv = sb("row_inv", [TILE, PER])
        t_now = sb("t_now", [TILE, PER, CHANNELS])

        xn2 = sb("xn2", [TILE, TILES, CHANNELS])
        xn2_now = sb("xn2_now", [TILE, PER, CHANNELS])
        xn2T = sb("xn2T", [CHANNELS, CHUNK])
        logit = sb("logit", [TILE, PER, EXPERTS])
        top8 = sb("top8", [TILE, PER, 8])
        top8_i = sb("top8_i", [TILE, PER, 8], u32)
        top_f = sb("top_f", [TILE, PER, TOP])
        pick1 = sb("pick1", [TILE, EXPERTS, TILES])
        pick2 = sb("pick2", [TILE, EXPERTS, TILES])
        gates = sb("gates", [TILE, 4, 2, TILES])
        gate_d = sb("gate_d", [TILE, PER])
        gate_e = sb("gate_e", [TILE, PER])
        picks = sb("picks", [TILE, EXPERTS, TILES])
        in_tile = sb("in_tile", [TILE, EXPERTS, TILES])
        upto = sb("upto", [TILE, EXPERTS, TILES])
        total_i = sb("total_i", [TILE, EXPERTS], i32)
        padded = sb("padded", [TILE, EXPERTS])
        run_end = sb("run_end", [TILE, EXPERTS])
        run_start = sb("run_start", [TILE, EXPERTS])
        tile_expert_f = sb("tile_expert_f", [TILE, SORTED_TILES])
        tile_expert = sb("tile_expert", [TILE, 4, SORTED_TILES], i32)
        slot_f = sb("slot_f", [TILE, TOP, TILES])
        slot = sb("slot", [TILE, 4, TOP, TILES], u32)
        row_now = sb("row_now", [TILE, PER, CHANNELS])
        slot_to = sb("slot_to", [TILE, TOP, PER], u32)
        slot_of = sb("slot_of", [TILE, TOP, PER], u32)

        fx = sb("fx", [SLOTS, SLICE, 2, CHANNELS])
        fx_hi = sb("fx_hi", [128, 2 * SLOTS], f32r)
        fx_lo = sb("fx_lo", [128, 2 * SLOTS], f32r)
        th = sb("th", [SLOTS, 2, HIDDEN])
        up = sb("up", [SLOTS, 2, HIDDEN])
        hid = sb("hid", [SLOTS, 2, HIDDEN])
        hidT = sb("hidT", [HIDDEN, 2 * SLOTS])
        fy = sb("fy", [SLOTS, SLICE, CHANNELS])
        got1 = sb("got1", [TILE, PER, CHANNELS])
        got2 = sb("got2", [TILE, PER, CHANNELS])
        tc = sb("tc", [TILE, PER, CHANNELS])
        t_out = sb("t_out", [TILE, PER, CHANNELS])
        out_s = sb("out_s", [CHANNELS, CHUNK])

        ps_s = [pb(f"ps_s{i}", [128, 512]) for i in range(2)]
        ps_m = [pb(f"ps_m{i}", [128, 512]) for i in range(2)]
        ps_o = pb("ps_o", [128, 512])
        ps_x = pb("ps_x", [128, 512])
        ps_y = pb("ps_y", [128, 512])
        ps_z = pb("ps_z", [128, 512])

        started = ctx.enter_context(nc.semaphore("started"))
        names = """weights_in w12_in w_twice wt_done wt_ready w_link bq_ready consts pool_chain
            w12_link w12_ready x_st_in stats_done gn_link gn_mean_ready gn_mean_done gn_dev_ready gn_var_done
            gn_var_ready gn_rstd_ready gn_scale_ready xh_in xg_ready xg_hi_ready xg_lo_ready border_ready
            conv_done xconv_ready tt_done tok_ready ln_link ln_var ln_rstd xn_ready xt_done v_ready xn_hi_ready
            xn_lo_ready q_done k_done q_f_ready k_f_ready qk_link q_ready k_ready
            qa_ready qmax_ready max_done max_red maxneg_ready shiftT_done shift_ready s_done p_ready pv_done
            z_ready outp_done o_link o_used t_out_dma
            ln2_link r_var r_rstd r_xn_ready r_t_done r_t_ready logit_done r_link logit_used gate_d_ready gate_e_ready
            gate_ready picks_ready total_done total_ready rank_done rank_ready rt_link slots_ready experts_ready
            slot_to_ready row_ready held scattered fx_in fx_t_done fx_hi_ready fx_lo_ready h_done th_ready f_link hid_ready ht_done
            ht_ready y_done fy_ready fy_out slot_of_ready gathered tc_in c_link c_ready c_t_done out_ready
            stored""".split()
        s = {n: ctx.enter_context(nc.semaphore(n)) for n in names}

        block = ctx.enter_context(nc.Block())

        def cols(c):
            return bass.ds(c * CHUNK, CHUNK)

        def tiles(c):
            return bass.ds(c * PER, PER)

        def wide(ap, shape):
            return ap.to_broadcast(shape)

        def halo(at):
            if at.static and at.c == 0:
                return slice(1, ROWS + 2)
            return slice(0, ROWS + 1 if at.static and at.c == CHUNKS - 1 else ROWS + 2)

        @block.sync
        def _(sp):
            sp.wait_ge(started, 1)
            for half in range(2):
                rows = slice(64 * half, 64 * half + 64)
                sp.dma_start(raw_w[rows, 0:TAPS * CHANNELS], conv_w).then_inc(s["weights_in"], 16)
                for m, w in enumerate((wq, wk, wv)):
                    to = (TAPS + m) * CHANNELS
                    sp.dma_start(raw_w[rows, to:to + CHANNELS], w).then_inc(s["weights_in"], 16)
                sp.dma_start(bq_raw[rows, :], bq.rearrange("(c a) -> c a", a=1)).then_inc(s["weights_in"], 16)
                sp.dma_start(bk_s[rows, :], bk.rearrange("(c a) -> c a", a=1)).then_inc(s["weights_in"], 16)
            sp.dma_start(w_out[CHANNELS:VCOLS, 0:CHANNELS], bv.rearrange("(a c) -> a c", a=1)).then_inc(s["weights_in"], 16)
            sp.dma_start(gate_bb[:], gate_b.rearrange("(a c) -> a c", a=1).partition_broadcast(TILE)
                         .rearrange("p a c -> p (a c)")).then_inc(s["weights_in"], 16)
            sp.dma_start(gate_s[:], gate_w).then_inc(s["weights_in"], 16)
            sp.dma_start(w3s[:], w3.rearrange("e h c -> h e c")).then_inc(s["weights_in"], 16)

            def load_halo(b, c, first, rows, count):
                wait_apart(sp, s["xconv_ready"], ONE + count)
                for half in range(2):
                    sp.dma_start(xh[64 * half:64 * half + 64, rows, :].rearrange("p h w -> p (h w)"),
                                 x_v[b, :, bass.ds(first * SIDE, (rows.stop - rows.start) * SIDE)])\
                        .then_inc(s["xh_in"], 16)

            def body(at, following=None):
                if at.active("stats"):
                    n = at.n + 2 * CHUNKS
                    wait_apart(sp, s["stats_done"], ONE + n)
                    for half in range(2):
                        sp.dma_start(x_st[64 * half:64 * half + 64, :], x_v[at.u + 2, :, cols(at.c)])\
                            .then_inc(s["x_st_in"], 16)
                if at.active("combine"):
                    k = at.index("combine")
                    wait_apart(sp, s["c_ready"], ONE + k)
                    sp.dma_start(tc[:].rearrange("p a c -> p (a c)"),
                                 kept[bass.ds(k, 1)].rearrange("a p c -> (a p) c")).then_inc(s["tc_in"], 16)
                if at.u == -2 and at.static and at.c == CHUNKS - 1:
                    load_halo(0, 0, 0, slice(1, ROWS + 2), 0)
                if at.u == -1:
                    for pair in [at.c, at.c + 1] if at.static and at.c == CHUNKS - 1 else [at.c]:
                        wait_apart(sp, s["w12_ready"], ONE + pair)
                        for half in range(2):
                            for m, w in enumerate((w1, w2)):
                                sp.dma_start((th, up)[m][64 * half:64 * half + 64],
                                             w[bass.ds(pair * 2, 2)].rearrange("e c h -> c e h")).then_inc(s["w12_in"], 16)
                if at.active("post"):
                    r = at.index("post")
                    wait_apart(sp, s["o_used"], ONE + r + 1)
                    sp.dma_start(kept[bass.ds(r, 1)].rearrange("a p c -> (a p) c"),
                                 t_now[:].rearrange("p a c -> p (a c)")).then_inc(s["t_out_dma"], 16)
                if at.active("pre") and following is not None:
                    b, c, rows = following
                    load_halo(b, c, c * ROWS - 1 if rows.start == 0 else 0, rows, at.index("pre") + 1)
                if at.active("combine"):
                    k = at.index("combine")
                    wait_apart(sp, s["out_ready"], ONE + k + 1)
                    sp.dma_start(out_v[at.batch("combine"), :, cols(at.chunk("combine"))], out_s[:]).then_inc(s["stored"], 16)
                if at.active("experts"):
                    f = at.index("experts")
                    wait_apart(sp, s["fy_ready"], ONE + (f + 1) * PAIRS)
                    if at.batch("experts") >= 2:
                        wait_apart(sp, s["gathered"], ZEROS + (at.batch("experts") - 1) * (16 * TOP * TILES))
                    sp.dma_start(sorted_y[at.batch("experts") % 2][bass.ds(at.chunk("experts") * (SLICE * SLOTS), SLICE * SLOTS)]
                                 .rearrange("(t p) c -> p t c", p=SLOTS), fy[:]).then_inc(s["fy_out"], 16)
                nxt = At(at.next_u, at.next_c) if at.static else None
                active, b, c, f = (at.active("experts"), at.batch("experts"), at.chunk("experts") + 1,
                                   at.index("experts") + 1) if nxt is None else \
                    (nxt.active("experts"), nxt.batch("experts"), nxt.chunk("experts"), nxt.index("experts"))
                if active:
                    wait_apart(sp, s["scattered"], ZEROS + (b + 1) * (16 * TOP * TILES))
                    wait_apart(sp, s["fx_t_done"], ONE + f * PAIRS)
                    for twice in range(2):
                        sp.dma_start(fx[:, :, twice, :], sorted_x[b % 2][bass.ds(c * (SLICE * SLOTS), SLICE * SLOTS)]
                                     .rearrange("(t p) c -> p t c", p=SLOTS)).then_inc(s["fx_in"], 16)

            everything = slice(0, ROWS + 2)
            for u in range(-2, BATCHES + 4):
                if u == BATCHES + 3:
                    body(At(u, 0))
                    break
                body(At(u, 0), (u + 1, 1, everything))
                with sp.Fori(1, CHUNKS - 2) as c:
                    body(At(u, c), (u + 1, c + 1, everything))
                five = At(u, CHUNKS - 2)
                body(five, (u + 1, CHUNKS - 1, slice(0, ROWS + 1)))
                body(At(u, CHUNKS - 1), (u + 2, 0, slice(1, ROWS + 2)) if u + 2 < BATCHES else None)
            sp.wait_ge(s["stored"], ONE + 16 * ALL)

        @block.gpsimd
        def _(pool):
            g = nc.gpsimd
            for n in names:
                if n not in ("scattered", "gathered"):
                    g.sem_inc(s[n], 1)
            g.sem_inc(started, 1)
            pool.wait_ge(started, 1)
            chain = Link(pool, s["pool_chain"], 0)
            chain(g.memset(ident[:], 0.0))
            chain(g.affine_select(out=ident[:], in_=ident[:], compare_op=ALU.not_equal, fill=1.0, base=0,
                                  pattern=[[-1, 128]], channel_multiplier=1))
            chain(g.memset(pair_mean[:], 0.5))
            pm = pair_mean[:].rearrange("p (j k) -> p j k", k=2)
            chain(g.affine_select(out=pm, in_=pm, compare_op=ALU.is_ge, fill=0.0, base=0,
                                  pattern=[[-2, 64], [0, 2]], channel_multiplier=1))
            chain(g.affine_select(out=pm, in_=pm, compare_op=ALU.is_ge, fill=0.0, base=1,
                                  pattern=[[2, 64], [0, 2]], channel_multiplier=-1))
            chain(g.memset(ones[:], 1.0))
            chain(g.affine_select(out=before[:], in_=ones[:], compare_op=ALU.is_gt, fill=0.0, base=0,
                                  pattern=[[1, TILE]], channel_multiplier=-1))
            chain(g.memset(minus_half[:], -0.5))
            chain(g.iota(expert_i[:], pattern=[[1, EXPERTS]], base=0, channel_multiplier=0))
            chain(g.iota(tile_i[:], pattern=[[SLOTS, SORTED_TILES]], base=0, channel_multiplier=0))
            chain(g.tensor_copy(expert_f[:], expert_i[:]))
            chain(g.tensor_copy(tile_f[:], tile_i[:]))
            chain(g.memset(not_first[:], 1.0))
            chain(g.memset(not_first[:].rearrange("p (e t) -> p e t", t=TILES)[:, :, 0:1], 0.0))
            for part in (xg_hi, xg_lo):
                chain(g.memset(part[:].bitcast(f32), 0.0))
            for p in range(2):
                chain(g.memset(v_s[p][:, :, CHANNELS:VCOLS], 1.0))
                chain(g.memset(k_b[p][:].bitcast(f32), 1.0))
            chain(g.memset(w_out[0:CHANNELS, CHANNELS:VCOLS], 0.0))
            chain(g.memset(fy[:], 0.0))
            g.memset(gn_q[:], 0.0).then_inc(s["consts"], 1)
            for p in range(2):
                for c in range(CHUNKS):
                    g.dma_start(sorted_x[p][c * SLICE * SLOTS:(c + 1) * SLICE * SLOTS]
                                .rearrange("(t p) c -> p t c", p=SLOTS), fy[:]).then_inc((s["scattered"], s["gathered"])[p], 16)
            pool.wait_ge(s["scattered"], ZEROS + 0)
            pool.wait_ge(s["gathered"], ZEROS + 0)

            def scatter(at):
                m, b = at.index("scatter"), at.batch("scatter")
                wait_apart(pool, s["slots_ready"], ONE + b + 1)
                wait_apart(pool, s["scattered"], ZEROS + m * (16 * TOP * PER))
                if b >= 2:
                    wait_apart(pool, s["fx_in"], ONE + (b - 1) * CHUNKS * 32)
                g.tensor_copy(slot_to[:], slot[:, b % 4, :, tiles(at.chunk("scatter"))]).then_inc(s["slot_to_ready"], 1)
                wait_apart(pool, s["slot_to_ready"], ONE + m + 1)
                wait_apart(pool, s["row_ready"], ONE + m + 1)
                for j in range(PER):
                    for k in range(TOP):
                        g.indirect_dma_start(
                            out=sorted_x[b % 2], out_offset=bass.IndirectOffsetOnAxis(ap=slot_to[:, k, j:j + 1], axis=0),
                            in_=row_now[:, j, :], in_offset=None).then_inc(s["scattered"], 16)

            def gather(at):
                k, b = at.index("combine"), at.batch("combine")
                wait_apart(pool, s["fy_out"], ONE + (b + 1) * CHUNKS * 16)
                wait_apart(pool, s["c_ready"], ONE + k)
                g.tensor_copy(slot_of[:], slot[:, b % 4, :, tiles(at.chunk("combine"))]).then_inc(s["slot_of_ready"], 1)
                wait_apart(pool, s["slot_of_ready"], ONE + k + 1)
                for j in range(PER):
                    for m, got in enumerate((got1, got2)):
                        g.indirect_dma_start(
                            out=got[:, j, :], out_offset=None, in_=sorted_y[b % 2],
                            in_offset=bass.IndirectOffsetOnAxis(ap=slot_of[:, m, j:j + 1], axis=0)).then_inc(s["gathered"], 16)

            def norm1(at):
                wait_apart(pool, s["ln_var"], ONE + at.index("pre") + 1)
                g.tensor_tensor(ln_s[:, 3, :], ln_s[:, 2, :], minus_half[0:TILE, :], ALU.pow).then_inc(s["ln_rstd"], 1)

            def norm2(at):
                wait_apart(pool, s["r_var"], ONE + at.index("post") + 1)
                g.tensor_tensor(ln_s[:, 3, :], ln_s[:, 2, :], minus_half[0:TILE, :], ALU.pow).then_inc(s["r_rstd"], 1)

            events = {"scatter": scatter, "gather": gather, "norm1": norm1, "norm2": norm2}

            def body(at):
                for _, stage, name in STEPS_POOL:
                    if name in events and at.active(stage):
                        events[name](at)
                if at.active("stats") and at.static and at.c == CHUNKS - 1:
                    wait_apart(pool, s["gn_var_ready"], ONE + at.u + 3)
                    g.tensor_tensor(gn_rstd[:], gn_var[:], minus_half[:, 0:1], ALU.pow).then_inc(s["gn_rstd_ready"], 1)

            iterations(pool, body)

        @block.scalar
        def _(act):
            a = nc.scalar
            act.wait_ge(started, 1)
            act.wait_ge(s["weights_in"], ONE + 16 * 16)
            a.mul(bq_s[:], bq_raw[:], 0.125).then_inc(s["bq_ready"], 1)
            act.wait_ge(s["bq_ready"], ONE + 1)

            def normed(at):
                n, rows = at.index("pre"), halo(at)
                act.wait_ge(s["gn_scale_ready"], ONE + at.batch("pre") + 1)
                act.wait_ge(s["xh_in"], ONE + (n + 1) * 32)
                act.wait_ge(s["xg_lo_ready"], ONE + n)
                a.activation(xg_f[:, rows, :], xh[:, rows, :], ACT.Identity, bias=gn_bias[:], scale=gn_rstd[:])\
                    .then_inc(s["xg_ready"], 1)

            def hold(at):
                wait_apart(act, s["o_used"], ONE + at.n)
                a.activation(tok_held[:], tok[:, tiles(at.c), :], ACT.Copy).then_inc(s["held"], 1)

            def tokens(at):
                n = at.index("pre")
                if at.attends:
                    act.wait_ge(s["held"], ONE + at.n + 1)
                wait_apart(act, s["tt_done"], ONE + n + 1)
                a.activation(tok[:, tiles(at.c), :],
                             ps_y[0:TILE, 0:PER * CHANNELS].rearrange("p (t c) -> p t c", c=CHANNELS), ACT.Copy)\
                    .then_inc(s["tok_ready"], 1)

            def turned(at):
                n = at.index("pre")
                act.wait_ge(s["xt_done"], ONE + n + 1)
                act.wait_ge(s["k_done"], ONE + n)
                a.activation(xn_hi[:], ps_y[:, 0:CHUNK], ACT.Copy).then_inc(s["xn_hi_ready"], 1)
                a.activation(v_s[at.batch("pre") % 2][:, tiles(at.c), 0:CHANNELS], xn[:, :, 0, :], ACT.Copy)\
                    .then_inc(s["v_ready"], 1)

            def query(at):
                n = at.index("pre")
                act.wait_ge(s["q_done"], ONE + n + 1)
                act.wait_ge(s["q_ready"], ONE + n)
                a.activation(qk_f[:, 0, :], ps_y[:, 0:CHUNK], ACT.Identity, bias=bq_s[:], scale=0.125)\
                    .then_inc(s["q_f_ready"], 1)

            def key(at):
                n = at.index("pre")
                act.wait_ge(s["k_done"], ONE + n + 1)
                act.wait_ge(s["k_ready"], ONE + n)
                a.activation(qk_f[:, 1, :], ps_y[:, 0:CHUNK], ACT.Identity, bias=bk_s[:], scale=1.0)\
                    .then_inc(s["k_f_ready"], 1)

            def turned2(at):
                r = at.index("post")
                act.wait_ge(s["r_t_done"], ONE + r + 1)
                act.wait_ge(s["logit_done"], ONE + r)
                a.activation(xn2T[:], ps_y[0:CHANNELS, 0:CHUNK], ACT.Copy).then_inc(s["r_t_ready"], 1)

            def gate(at):
                r = at.index("post")
                act.wait_ge(s["gate_d_ready"], ONE + r + 1)
                act.wait_ge(s["gate_ready"], ONE + r)
                a.activation(gate_e[:], gate_d[:], ACT.Exp).then_inc(s["gate_e_ready"], 1)

            def combine(at):
                k = at.index("combine")
                act.wait_ge(s["c_t_done"], ONE + k + 1)
                act.wait_ge(s["stored"], ONE + k * 16)
                a.activation(out_s[:], ps_y[0:CHANNELS, 0:CHUNK], ACT.Copy).then_inc(s["out_ready"], 1)

            def expert(at, name, pair):
                f = at.index("experts") * PAIRS + pair
                if name == "fx":
                    act.wait_ge(s["fx_t_done"], ONE + f + 1)
                    act.wait_ge(s["h_done"], ONE + f)
                    a.activation(fx_hi[:], ps_z[:, 0:2 * SLOTS], ACT.Copy).then_inc(s["fx_hi_ready"], 1)
                elif name == "hidden":
                    act.wait_ge(s["h_done"], ONE + f + 1)
                    act.wait_ge(s["hid_ready"], ONE + f)
                    a.activation(th[:], ps_x[:].rearrange("p (t m h) -> p t m h", t=2, m=2)[:, :, 0, :],
                                 ACT.Tanh, scale=0.5).then_inc(s["th_ready"], 1)
                elif name == "turn":
                    act.wait_ge(s["ht_done"], ONE + f + 1)
                    act.wait_ge(s["y_done"], ONE + f)
                    a.activation(hidT[:], ps_z[:, 0:2 * SLOTS], ACT.Copy).then_inc(s["ht_ready"], 1)
                else:
                    act.wait_ge(s["y_done"], ONE + f + 1)
                    if pair == 0:
                        act.wait_ge(s["fy_out"], ONE + at.index("experts") * 16)
                    a.activation(fy[:, 2 * pair:2 * pair + 2, :],
                                 ps_x[:, 0:2 * CHANNELS].rearrange("p (t c) -> p t c", c=CHANNELS),
                                 ACT.Copy, scale=0.5).then_inc(s["fy_ready"], 1)

            events = {"normed": normed, "hold": hold, "tokens": tokens, "turned": turned, "query": query, "key": key,
                      "turned2": turned2, "gate": gate, "combine": combine}

            def next_queries(n):
                act.wait_ge(s["qa_ready"], ONE + n + 1)
                wait_apart(act, s["max_done"], ONE + n * TILES)
                a.activation(q_max[:], q_a[:, bass.ds(n % 2, 1), :].rearrange("p a c -> p (a c)").bitcast(f32), ACT.Copy)\
                    .then_inc(s["qmax_ready"], 1)

            def next_shift(n):
                wait_apart(act, s["shiftT_done"], ONE + n + 1)
                a.activation(q_b[64:65, bass.ds(n % 2, 1), :].rearrange("p a c -> p (a c)"), ps_y[64:65, 0:CHUNK], ACT.Copy)\
                    .then_inc(s["shift_ready"], 1)

            def body(at):
                if at.active("post"):
                    act.wait_ge(s["pv_done"], ONE + at.index("post") * TILES + TILES)
                    act.wait_ge(s["outp_done"], ONE + at.index("post"))
                    a.activation(z_s[:], ps_o[0:VCOLS, 0:CHUNK], ACT.Copy).then_inc(s["z_ready"], 1)
                for i in range(TILES):
                    if at.attends:
                        act.wait_ge(s["s_done"], ONE + at.n * TILES + (i + 1))
                        a.activation(prob[i % 4][:], ps_s[i % 2][0:TILE, 0:CHUNK], ACT.Exp).then_inc(s["p_ready"], 1)
                    for step, stage, name in STEPS:
                        if step == i and name in events and at.active(stage):
                            events[name](at)
                    for step, name, pair in EXPERT_STEPS:
                        if step == i and at.active("experts"):
                            expert(at, name, pair)
                    if i == NEXT_QUERIES and at.ahead:
                        next_queries(at.n + 1)
                    if i == TILES - 1 and at.ahead:
                        next_shift(at.n + 1)
                if at.u == -1 and at.static and at.c == CHUNKS - 1:
                    next_queries(0)
                    next_shift(0)

            iterations(act, body)

        @block.vector
        def _(dve):
            v = nc.vector
            dve.wait_ge(started, 1)
            dve.wait_ge(s["weights_in"], ONE + 16 * 16)
            dve.wait_ge(s["consts"], ONE + 1)
            taps = raw_w[:, 0:TAPS * CHANNELS].rearrange("p (c k) -> p k c", k=TAPS)
            twice = xg_f[:].rearrange("p h w -> p (h w)")[:, 0:512]
            hi = k_a[0][:, 0:512]
            for g in range(3):
                for m in range(4 * g, 4 * g + 4):
                    w = taps[:, m, :] if m < TAPS else raw_w[:, m * CHANNELS:(m + 1) * CHANNELS]
                    last = v.tensor_copy(twice[:, m % 4 * 128:m % 4 * 128 + 128].rearrange("p (a b) -> p a b", a=2),
                                         w.unsqueeze(1).to_broadcast([128, 2, CHANNELS]))
                last.then_inc(s["w_twice"], 1)
                dve.wait_ge(s["wt_done"], ONE + g + 1)
                many = 4 if g < 2 else 3
                to = wT[:, 4 * g:4 * g + many, :].rearrange("p a b -> p (a b)")
                v.tensor_copy(to[0:64, :], ps_x[0:64, 0:128 * many])
                v.tensor_copy(hi[64:128, 0:128 * many], ps_x[64:128, 0:128 * many]).then_inc(s["w_link"], 1)
                dve.wait_ge(s["w_link"], ONE + g + 1)
                if g == 2:
                    v.tensor_copy(w_out[0:CHANNELS, 0:CHANNELS], ps_x[0:64, 384:448])
                    v.memset(w_out[CHANNELS:VCOLS, CHANNELS:VCOLS], 1.0)
                v.tensor_tensor(to[64:128, :], ps_x[64:128, 0:128 * many], hi[64:128, 0:128 * many].bitcast(f32),
                                ALU.subtract).then_inc(s["wt_ready"], 1)
                dve.wait_ge(s["wt_ready"], ONE + g + 1)

            def expert_weights(pair, keys):
                dve.wait_ge(s["w12_in"], ONE + (pair + 1) * 4 * 16)
                dve.wait_ge(s["k_ready"], ONE + keys)
                for m, raw in enumerate((th, up)):
                    to = w12[:, bass.ds(pair * 2, 2), m * HIDDEN:(m + 1) * HIDDEN]
                    hi = qk_hi[:, 0:2 * HIDDEN].rearrange("p (e h) -> p e h", h=HIDDEN)
                    v.tensor_copy(to[0:64], raw[0:64])
                    v.tensor_copy(hi[64:128], raw[64:128]).then_inc(s["w12_link"], 1)
                    dve.wait_ge(s["w12_link"], ONE + pair * 3 + 2 * m + 1)
                    last = v.tensor_tensor(to[64:128], raw[64:128], hi[64:128].bitcast(f32), ALU.subtract)
                    if m == 0:
                        last.then_inc(s["w12_link"], 1)
                        dve.wait_ge(s["w12_link"], ONE + pair * 3 + 2)
                last.then_inc(s["w12_ready"], 1)
                dve.wait_ge(s["w12_ready"], ONE + pair + 1)

            def layer_norm(link, source, var_sem, rstd_sem, n):
                link(v.tensor_reduce(ln_s[:, 0, :], source, AX.X, ALU.add))
                link(v.tensor_scalar(ln_s[:, 1, :], ln_s[:, 0, :], 1.0 / CHANNELS, None, ALU.mult))
                link(v.tensor_tensor(ln_c[:], source, ln_s[:, 1, :].unsqueeze(2).to_broadcast([TILE, PER, CHANNELS]),
                                     ALU.subtract))
                link(v.tensor_tensor(ln_q[:], ln_c[:], ln_c[:], ALU.mult))
                link(v.tensor_reduce(ln_s[:, 1, :], ln_q[:], AX.X, ALU.add))
                v.tensor_scalar(ln_s[:, 2, :], ln_s[:, 1, :], 1.0 / CHANNELS, LN_EPS, ALU.mult, ALU.add)\
                    .then_inc(s[var_sem], 1)
                dve.wait_ge(s[rstd_sem], ONE + n + 1)

            def stats(at):
                n = at.n + 2 * CHUNKS
                dve.wait_ge(s["x_st_in"], ONE + (n + 1) * 32)
                v.bn_stats(gn_stats[:, bass.ds(at.c, 1), :].rearrange("p a b -> p (a b)"), x_st[:]).then_inc(s["stats_done"], 1)
                if not (at.static and at.c == CHUNKS - 1):
                    return
                b = at.u + 2
                wait_apart(dve, s["stats_done"], ONE + (b + 1) * CHUNKS)
                link = Link(dve, s["gn_link"], b * 4)
                v.bn_aggr(gn_mv[:], gn_stats[:].rearrange("p a b -> p (a b)")).then_inc(s["gn_mean_ready"], 1)
                dve.wait_ge(s["gn_mean_done"], ONE + b + 1)
                link(v.tensor_copy(gn_mean[:], ps_y[:, 0:1]))
                link(v.tensor_tensor(gn_d[:], gn_mv[:, 0:1], gn_mean[:], ALU.subtract))
                link(v.tensor_tensor(gn_q[:], gn_d[:], gn_d[:], ALU.mult))
                v.tensor_tensor(gn_e[:], gn_mv[:, 1:2], gn_q[:], ALU.add).then_inc(s["gn_dev_ready"], 1)
                dve.wait_ge(s["gn_var_done"], ONE + b + 1)
                v.tensor_scalar(gn_var[:], ps_y[:, 1:2], GN_EPS, None, ALU.add).then_inc(s["gn_var_ready"], 1)
                dve.wait_ge(s["gn_rstd_ready"], ONE + b + 1)
                link(v.tensor_tensor(gn_q[:], gn_mean[:], gn_rstd[:], ALU.mult))
                v.tensor_scalar(gn_bias[:], gn_q[:], -1.0, None, ALU.mult).then_inc(s["gn_scale_ready"], 1)

            def normed(at):
                n, rows = at.index("pre"), halo(at)
                dve.wait_ge(s["xg_ready"], ONE + n + 1)
                dve.wait_ge(s["conv_done"], ONE + n)
                inner = (slice(None), rows, slice(1, 1 + SIDE))
                v.tensor_copy(xg_hi[inner], xg_f[:, rows, :]).then_inc(s["xg_hi_ready"], 1)
                if at.static:
                    edge = 0 if at.c == 0 else ROWS + 1
                    for part in (xg_hi, xg_lo):
                        last = v.memset(part[:, edge:edge + 1, :].bitcast(f32), 0.0)
                    last.then_inc(s["border_ready"], 1)
                dve.wait_ge(s["xg_hi_ready"], ONE + n + 1)
                v.tensor_tensor(xg_lo[inner], xg_f[:, rows, :], xg_hi[inner].bitcast(f32), ALU.subtract)\
                    .then_inc(s["xg_lo_ready"], 1)

            def conv(at):
                n = at.index("pre")
                dve.wait_ge(s["conv_done"], ONE + n + 1)
                dve.wait_ge(s["tt_done"], ONE + n)
                v.tensor_tensor(x_conv[:], ps_z[0:CHANNELS, 0:CHUNK],
                                xh[0:CHANNELS, 1:ROWS + 1, :].rearrange("p h w -> p (h w)"), ALU.add)\
                    .then_inc(s["xconv_ready"], 1)

            def norm1(at):
                n = at.index("pre")
                dve.wait_ge(s["tok_ready"], ONE + n + 1)
                layer_norm(Link(dve, s["ln_link"], n * 5), tok[:, tiles(at.c), :], "ln_var", "ln_rstd", n)
                dve.wait_ge(s["xt_done"], ONE + n)
                dve.wait_ge(s["v_ready"], ONE + n)
                v.tensor_tensor(xn[:], ln_c[:].unsqueeze(2).to_broadcast([TILE, PER, 2, CHANNELS]),
                                ln_s[:, 3, :].unsqueeze(2).unsqueeze(3).to_broadcast([TILE, PER, 2, CHANNELS]),
                                ALU.mult).then_inc(s["xn_ready"], 1)

            def turned(at):
                n = at.index("pre")
                dve.wait_ge(s["xn_hi_ready"], ONE + n + 1)
                v.tensor_tensor(xn_lo[:], ps_y[:, 0:CHUNK], xn_hi[:].bitcast(f32), ALU.subtract).then_inc(s["xn_lo_ready"], 1)

            def query(at):
                n, to = at.index("pre"), q_hl
                dve.wait_ge(s["q_f_ready"], ONE + n + 1)
                v.tensor_copy(to[0:64, cols(at.c)], qk_f[0:64, 0, :])
                v.tensor_copy(qk_hi[64:128, :], qk_f[64:128, 0, :]).then_inc(s["qk_link"], 1)
                dve.wait_ge(s["qk_link"], ONE + n * 2 + 1)
                v.tensor_tensor(to[64:128, cols(at.c)], qk_f[64:128, 0, :], qk_hi[64:128, :].bitcast(f32),
                                ALU.subtract).then_inc(s["q_ready"], 1)

            def key(at):
                n, p = at.index("pre"), at.batch("pre") % 2
                dve.wait_ge(s["k_f_ready"], ONE + n + 1)
                dve.wait_ge(s["q_ready"], ONE + n + 1)
                v.tensor_copy(k_a[p][0:64, cols(at.c)], qk_f[0:64, 1, :])
                v.tensor_copy(k_b[p][0:64, cols(at.c)], qk_f[0:64, 1, :])
                v.tensor_copy(qk_hi[64:128, :], qk_f[64:128, 1, :]).then_inc(s["qk_link"], 1)
                dve.wait_ge(s["qk_link"], ONE + n * 2 + 2)
                v.tensor_tensor(k_a[p][64:128, cols(at.c)], qk_f[64:128, 1, :], qk_hi[64:128, :].bitcast(f32),
                                ALU.subtract).then_inc(s["k_ready"], 1)

            def next_queries(n, c):
                dve.wait_ge(s["q_ready"], ONE + n + 1)
                if not isinstance(n, int) or n:
                    dve.wait_ge(s["s_done"], ONE + (n - 1) * TILES)
                here = bass.ds(n % 2, 1)
                flat = lambda ap: ap.rearrange("p a c -> p (a c)")
                v.tensor_copy(flat(q_b[0:64, here, :]), q_hl[64:128, cols(c)].bitcast(f32))
                v.tensor_copy(flat(q_a[0:64, here, :]), q_hl[0:64, cols(c)].bitcast(f32))
                v.tensor_copy(flat(q_a[64:128, here, :]), q_hl[0:64, cols(c)].bitcast(f32)).then_inc(s["qa_ready"], 1)

            def reduces(n, which):
                for m in which:
                    dve.wait_ge(s["max_done"], ONE + n * TILES + (m + 1))
                    v.tensor_reduce(max_part[:, m // CHUNKS, m % CHUNKS:m % CHUNKS + 1],
                                    ps_m[m % 2][0:TILE, 0:CHUNK], AX.X, ALU.max).then_inc(s["max_red"], 1)

            def max_total(n):
                dve.wait_ge(s["max_red"], ONE + (n + 1) * TILES)
                dve.wait_ge(s["shiftT_done"], ONE + n)
                v.tensor_reduce(max_neg[:], max_part[:], AX.X, ALU.max, negate=True).then_inc(s["maxneg_ready"], 1)

            def attended(at):
                r = at.index("post")
                dve.wait_ge(s["outp_done"], ONE + r + 1)
                dve.wait_ge(s["t_out_dma"], ONE + r * 16)
                dve.wait_ge(s["held"], ONE + r + 1)
                o = ps_y[0:TILE, 0:PER * VCOLS].rearrange("p (t c) -> p t c", c=VCOLS)
                v.reciprocal(row_inv[:], o[:, :, CHANNELS]).then_inc(s["o_link"], 1)
                dve.wait_ge(s["o_link"], ONE + r + 1)
                for j in range(PER):
                    last = v.scalar_tensor_tensor(
                        out=t_now[:, j, :], in0=o[:, j, 0:CHANNELS], scalar=row_inv[:, j:j + 1],
                        in1=tok_held[:, j, :],
                        op0=ALU.mult, op1=ALU.add)
                last.then_inc(s["o_used"], 1)

            def rows(at):
                m = at.index("scatter")
                dve.wait_ge(s["scattered"], ZEROS + m * (16 * TOP * PER))
                v.tensor_copy(row_now[:], xn2[:, tiles(at.chunk("scatter")), :]).then_inc(s["row_ready"], 1)

            def norm2(at):
                r = at.index("post")
                dve.wait_ge(s["o_used"], ONE + r + 1)
                layer_norm(Link(dve, s["ln2_link"], r * 5), t_now[:], "r_var", "r_rstd", r)
                for to in (xn2[:, tiles(at.chunk("post")), :], xn2_now[:]):
                    last = v.tensor_tensor(to, ln_c[:], ln_s[:, 3, :].unsqueeze(2).to_broadcast([TILE, PER, CHANNELS]),
                                           ALU.mult)
                last.then_inc(s["r_xn_ready"], 1)

            def gate(at):
                r, b, here = at.index("post"), at.batch("post"), tiles(at.chunk("post"))
                dve.wait_ge(s["logit_done"], ONE + r + 1)
                link = Link(dve, s["r_link"], r * 6)
                v.tensor_tensor(logit[:], ps_y[0:TILE, 0:PER * EXPERTS].rearrange("p (t e) -> p t e", e=EXPERTS),
                                gate_bb[:].unsqueeze(1).to_broadcast([TILE, PER, EXPERTS]), ALU.add)\
                    .then_inc(s["logit_used"], 1)
                wait_apart(dve, s["logit_used"], ONE + r + 1)
                for j in range(PER):
                    last = v.max(top8[:, j, :], logit[:, j, :])
                link(last, True)
                for j in range(PER):
                    last = v.max_index(top8_i[:, j, :], top8[:, j, :], logit[:, j, :])
                v.tensor_tensor(gate_d[:], top8[:, :, 1], top8[:, :, 0], ALU.subtract).then_inc(s["gate_d_ready"], 1)
                link(last)
                link(v.tensor_copy(top_f[:], top8_i[:, :, 0:TOP]))
                for m, pick in enumerate((pick1, pick2)):
                    last = v.tensor_tensor(pick[:, :, here].rearrange("p e t -> p t e"),
                                           expert_f[:].unsqueeze(1).to_broadcast([TILE, PER, EXPERTS]),
                                           top_f[:, :, m:m + 1].to_broadcast([TILE, PER, EXPERTS]), ALU.is_equal)
                link(last)
                dve.wait_ge(s["gate_e_ready"], ONE + r + 1)
                link(v.tensor_scalar(gate_d[:], gate_e[:], 1.0, None, ALU.add))
                link(v.reciprocal(gates[:, b % 4, 0, here], gate_d[:]))
                v.tensor_tensor(gates[:, b % 4, 1, here], gate_e[:], gates[:, b % 4, 0, here], ALU.mult)\
                    .then_inc(s["gate_ready"], 1)

            flat3 = lambda t: t[:].rearrange("p e t -> p (e t)")

            def route_pick(b):
                dve.wait_ge(s["gate_ready"], ONE + (b + 1) * CHUNKS)
                v.tensor_tensor(picks[:], pick1[:], pick2[:], ALU.add).then_inc(s["picks_ready"], 1)
                dve.wait_ge(s["total_done"], ONE + b + 1)
                v.tensor_copy(flat3(in_tile), ps_y[0:TILE, 0:EXPERTS * TILES]).then_inc(s["total_ready"], 1)
                dve.wait_ge(s["total_ready"], ONE + b + 1)

            def route_rank(b, link):
                link(v.tensor_tensor_scan(flat3(upto), not_first[:], flat3(in_tile), 0.0, ALU.mult, ALU.add))
                link(v.tensor_scalar(total_i[:], upto[:, :, TILES - 1], float(SLOTS - 1), None, ALU.add))
                link(v.tensor_tensor(upto[:], upto[:], in_tile[:], ALU.subtract))
                dve.wait_ge(s["rank_done"], ONE + b + 1)
                v.tensor_tensor(flat3(upto), flat3(upto), ps_y[0:TILE, 0:EXPERTS * TILES], ALU.add).then_inc(s["rank_ready"], 1)
                dve.wait_ge(s["rank_ready"], ONE + b + 1)

            def route_runs(b, link):
                shift = SLOTS.bit_length() - 1
                link(v.tensor_scalar(total_i[:], total_i[:], shift, shift, ALU.arith_shift_right, ALU.arith_shift_left))
                link(v.tensor_copy(padded[:], total_i[:]))
                link(v.tensor_tensor_scan(run_end[:], ones[:, 0:EXPERTS], padded[:], 0.0, ALU.mult, ALU.add))
                link(v.tensor_tensor(run_start[:], run_end[:], padded[:], ALU.subtract))

            def route_start(b, link):
                link(v.tensor_tensor(upto[:], upto[:], run_start[:].unsqueeze(2).to_broadcast([TILE, EXPERTS, TILES]), ALU.add))

            def route_slot(b, link, m):
                link(v.tensor_tensor(picks[:], (pick1, pick2)[m][:], upto[:], ALU.mult))
                link(v.tensor_reduce(slot_f[:, m, :], picks[:].rearrange("p e t -> p t e"), AX.X, ALU.add))

            def route_slots(b, link):
                v.tensor_copy(slot[:, b % 4, :, :], slot_f[:]).then_inc(s["slots_ready"], 1)
                dve.wait_ge(s["slots_ready"], ONE + b + 1)

            def route_experts(b, link, part):
                share = SORTED_TILES // 5
                these = slice(part * share, (part + 1) * share)
                ended = flat3(picks)[:, 0:share * EXPERTS].rearrange("p (j e) -> p j e", e=EXPERTS)
                link(v.tensor_tensor(ended, run_end[:].unsqueeze(1).to_broadcast([TILE, share, EXPERTS]),
                                     tile_f[:, these].unsqueeze(2).to_broadcast([TILE, share, EXPERTS]), ALU.is_le))
                link(v.tensor_reduce(tile_expert_f[:, these], ended, AX.X, ALU.add))
                if part == 4:
                    v.tensor_scalar(tile_expert[:, b % 4, :], tile_expert_f[:], float(EXPERTS - 1), None, ALU.min)\
                        .then_inc(s["experts_ready"], 1)

            ROUTE = {12: route_rank, 13: route_runs, 14: route_start, 16: lambda b, l: route_slot(b, l, 0),
                     17: lambda b, l: route_slot(b, l, 1), 18: route_slots,
                     **{19 + k: (lambda b, l, k=k: route_experts(b, l, k)) for k in range(5)}}
            route_links = {}

            def expert(at, name, pair):
                f = at.index("experts") * PAIRS + pair
                if name == "fx":
                    dve.wait_ge(s["fx_hi_ready"], ONE + f + 1)
                    v.tensor_tensor(fx_lo[:], ps_z[:, 0:2 * SLOTS], fx_hi[:].bitcast(f32), ALU.subtract)\
                        .then_inc(s["fx_lo_ready"], 1)
                elif name == "hidden":
                    dve.wait_ge(s["th_ready"], ONE + f + 1)
                    both = ps_x[:].rearrange("p (t m h) -> p t m h", t=2, m=2)
                    v.scalar_tensor_tensor(out=up[:], in0=th[:], scalar=1.0, in1=both[:, :, 0, :],
                                           op0=ALU.add, op1=ALU.mult).then_inc(s["f_link"], 1)
                    dve.wait_ge(s["f_link"], ONE + f + 1)
                    dve.wait_ge(s["ht_done"], ONE + f)
                    v.tensor_tensor(hid[:], up[:], both[:, :, 1, :], ALU.mult).then_inc(s["hid_ready"], 1)

            def combine(at):
                k, b = at.index("combine"), at.batch("combine")
                dve.wait_ge(s["gathered"], ZEROS + (k + 1) * (16 * TOP * PER))
                dve.wait_ge(s["tc_in"], ONE + (k + 1) * 16)
                link = Link(dve, s["c_link"], k * 2)
                for m, got in enumerate((got1, got2)):
                    last = v.tensor_tensor(got[:], got[:], gates[:, b % 4, m, tiles(at.chunk("combine"))].unsqueeze(2)
                                           .to_broadcast([TILE, PER, CHANNELS]), ALU.mult)
                link(last)
                link(v.tensor_tensor(got1[:], got1[:], got2[:], ALU.add))
                dve.wait_ge(s["c_t_done"], ONE + k)
                v.tensor_tensor(t_out[:], tc[:], got1[:], ALU.add).then_inc(s["c_ready"], 1)

            events = {"normed": normed, "conv": conv, "norm1": norm1, "turned": turned, "query": query, "key": key,
                      "attended": attended, "rows": rows, "norm2": norm2, "gate": gate, "combine": combine,
                      "stats": stats}

            def body(at):
                routes = at.static and at.c == 0 and at.active("post")
                b = at.batch("post")
                done = 0
                link = Link(dve, s["rt_link"], b * 22)
                for i in range(TILES):
                    if at.ahead:
                        reach = max_reach(i)
                        reduces(at.n + 1, range(done, reach))
                        done = reach
                    for step, stage, name in STEPS:
                        if step == i and name in events and at.active(stage):
                            events[name](at)
                    for step, name, pair in EXPERT_STEPS:
                        if step == i and at.active("experts"):
                            expert(at, name, pair)
                    if routes and i == 11:
                        route_pick(b)
                    if routes and i in ROUTE:
                        ROUTE[i](b, link)
                    if i == NEXT_QUERIES and at.ahead:
                        next_queries(at.n + 1, at.next_c)
                    if i == TILES - 1 and at.ahead:
                        max_total(at.n + 1)
                assert not routes or link.count == 22, link.count
                if at.u == -1:
                    for pair in [at.c, at.c + 1] if at.static and at.c == CHUNKS - 1 else [at.c]:
                        expert_weights(pair, at.index("pre") + 1)
                    if at.static and at.c == CHUNKS - 1:
                        next_queries(0, 0)
                        reduces(0, range(TILES))
                        max_total(0)

            iterations(dve, body)

        @block.tensor
        def _(pe):
            t = nc.tensor
            pe.wait_ge(started, 1)
            pe.wait_ge(s["consts"], ONE + 1)
            twice = xg_f[:].rearrange("p h w -> p (h w)")
            for m in range(TAPS + 3):
                if m % 4 == 0:
                    pe.wait_ge(s["w_twice"], ONE + m // 4 + 1)
                    pe.wait_ge(s["wt_ready"], ONE + m // 4)
                last = t.transpose(ps_x[:, 128 * (m % 4):128 * (m % 4) + 128], twice[:, m % 4 * 128:m % 4 * 128 + 128], ident[:])
                if m % 4 == 3:
                    last.then_inc(s["wt_done"], 1)
            pe.wait_ge(s["wt_ready"], ONE + 3)

            def maxima(n, u, which):
                for m in which:
                    if m == 0:
                        pe.wait_ge(s["qmax_ready"], ONE + n + 1)
                    if m >= 2:
                        pe.wait_ge(s["max_red"], ONE + n * TILES + (m - 1))
                    j, kb = m // CHUNKS, m % CHUNKS
                    if kb == CHUNKS - 1 and j == 0:
                        pe.wait_ge(s["k_ready"], ONE + (u + 1) * CHUNKS)
                    t.matmul(ps_m[m % 2][0:TILE, 0:CHUNK], q_max[:, j * TILE:(j + 1) * TILE],
                             k_a[u % 2][:, kb * CHUNK:(kb + 1) * CHUNK], start=True, stop=True).then_inc(s["max_done"], 1)

            def shift(n):
                pe.wait_ge(s["maxneg_ready"], ONE + n + 1)
                for j in range(PER):
                    last = t.transpose(ps_y[:, j * TILE:(j + 1) * TILE],
                                       max_neg[:, j:j + 1].to_broadcast([TILE, 128]), ident[0:TILE, 0:TILE])
                last.then_inc(s["shiftT_done"], 1)

            def scores(at, i):
                p = at.u % 2
                if i == 0:
                    pe.wait_ge(s["shift_ready"], ONE + at.n + 1)
                    pe.wait_ge(s["v_ready"], ONE + (at.u + 1) * CHUNKS)
                if i >= 2:
                    pe.wait_ge(s["p_ready"], ONE + at.n * TILES + (i - 1))
                keys, now = slice(i * TILE, (i + 1) * TILE), bass.ds(at.n % 2, 1)
                t.matmul(ps_s[i % 2][0:TILE, 0:CHUNK], k_a[p][:, keys], q_a[:, now, :].rearrange("p a c -> p (a c)"),
                         start=True, stop=False)
                t.matmul(ps_s[i % 2][0:TILE, 0:CHUNK], k_b[p][0:65, keys], q_b[0:65, now, :].rearrange("p a c -> p (a c)"),
                         start=False, stop=True).then_inc(s["s_done"], 1)

            def weigh(at, i):
                if i == 0:
                    pe.wait_ge(s["z_ready"], ONE + at.n)
                pe.wait_ge(s["p_ready"], ONE + at.n * TILES + (i + 1))
                t.matmul(ps_o[0:VCOLS, 0:CHUNK], v_s[at.u % 2][:, i, :], prob[i % 4][:], start=(i == 0),
                         stop=(i == TILES - 1)).then_inc(s["pv_done"], 1)

            class Bank:

                def __init__(self):
                    self.readers = []

                def take(self, *readers):
                    for name, count in self.readers:
                        wait_apart(pe, s[name], ONE + count)
                    self.readers = list(readers)

            bank_x, bank_y, bank_z = Bank(), Bank(), Bank()

            def conv(at):
                n = at.index("pre")
                bank_z.take(("xconv_ready", n + 1))
                pe.wait_ge(s["xg_lo_ready"], ONE + n + 1)
                for k in range(TAPS):
                    for part in (xg_hi, xg_lo):
                        last = t.matmul(ps_z[:, 0:CHUNK], wT[:, k, :], part[:, k // 3:k // 3 + ROWS, k % 3:k % 3 + SIDE],
                                        start=(k == 0 and part is xg_hi), stop=(k == TAPS - 1 and part is xg_lo))
                last.then_inc(s["conv_done"], 1)

            def tokens(at):
                n = at.index("pre")
                bank_y.take(("tok_ready", n + 1))
                wait_apart(pe, s["xconv_ready"], ONE + n + 1)
                for j in range(PER):
                    last = t.transpose(ps_y[0:TILE, j * CHANNELS:(j + 1) * CHANNELS], x_conv[:, j * TILE:(j + 1) * TILE],
                                       ident[0:CHANNELS, 0:CHANNELS])
                last.then_inc(s["tt_done"], 1)

            def turned(at):
                n = at.index("pre")
                bank_y.take(("xn_lo_ready", n + 1))
                pe.wait_ge(s["xn_ready"], ONE + n + 1)
                for j in range(PER):
                    last = t.transpose(ps_y[:, j * TILE:(j + 1) * TILE], xn[:, j, :, :].rearrange("p a b -> p (a b)"),
                                       ident[0:TILE, 0:TILE])
                last.then_inc(s["xt_done"], 1)

            def project(at, m, ready, done):
                bank_y.take((ready, at.index("pre") + 1))
                t.matmul(ps_y[:, 0:CHUNK], wT[:, TAPS + m, :], xn_hi[:], start=True, stop=False)
                t.matmul(ps_y[:, 0:CHUNK], wT[:, TAPS + m, :], xn_lo[:], start=False, stop=True).then_inc(s[done], 1)

            def attended(at):
                r = at.index("post")
                bank_y.take(("o_used", r + 1))
                pe.wait_ge(s["z_ready"], ONE + r + 1)
                for j in range(PER):
                    last = t.matmul(ps_y[0:TILE, j * VCOLS:(j + 1) * VCOLS], z_s[:, j * TILE:(j + 1) * TILE], w_out[:],
                                    start=True, stop=True)
                last.then_inc(s["outp_done"], 1)

            def turned2(at):
                r = at.index("post")
                bank_y.take(("r_t_ready", r + 1))
                wait_apart(pe, s["r_xn_ready"], ONE + r + 1)
                for j in range(PER):
                    last = t.transpose(ps_y[0:CHANNELS, j * TILE:(j + 1) * TILE], xn2_now[:, j, :], ident[0:TILE, 0:TILE])
                last.then_inc(s["r_t_done"], 1)

            def gate(at):
                r = at.index("post")
                bank_y.take(("logit_used", r + 1))
                for j in range(PER):
                    last = t.matmul(ps_y[0:TILE, j * EXPERTS:(j + 1) * EXPERTS], xn2T[:, j * TILE:(j + 1) * TILE],
                                    gate_s[:], start=True, stop=True)
                last.then_inc(s["logit_done"], 1)

            def combine(at):
                k = at.index("combine")
                bank_y.take(("out_ready", k + 1))
                wait_apart(pe, s["c_ready"], ONE + k + 1)
                for j in range(PER):
                    last = t.transpose(ps_y[0:CHANNELS, j * TILE:(j + 1) * TILE], t_out[:, j, :], ident[0:TILE, 0:TILE])
                last.then_inc(s["c_t_done"], 1)

            def stats(at):
                if not (at.static and at.c == CHUNKS - 1):
                    return
                b = at.u + 2
                bank_y.take(("gn_var_ready", b + 1))
                pe.wait_ge(s["gn_mean_ready"], ONE + b + 1)
                t.matmul(ps_y[:, 0:1], pair_mean[:], gn_mv[:, 0:1], start=True, stop=True).then_inc(s["gn_mean_done"], 1)
                pe.wait_ge(s["gn_dev_ready"], ONE + b + 1)
                t.matmul(ps_y[:, 1:2], pair_mean[:], gn_e[:], start=True, stop=True).then_inc(s["gn_var_done"], 1)

            flat_picks = picks[:].rearrange("p e t -> p (e t)")

            def route_total(b):
                bank_y.take(("total_ready", b + 1))
                pe.wait_ge(s["picks_ready"], ONE + b + 1)
                t.matmul(ps_y[0:TILE, 0:EXPERTS * TILES], ones[:], flat_picks, start=True, stop=True).then_inc(s["total_done"], 1)

            def route_rank(b):
                bank_y.take(("rank_ready", b + 1))
                t.matmul(ps_y[0:TILE, 0:EXPERTS * TILES], before[:], flat_picks, start=True, stop=True).then_inc(s["rank_done"], 1)

            picked = {}

            def expert(at, name, pair):
                f = at.index("experts") * PAIRS + pair
                if name == "fx":
                    if pair == 0:
                        pe.wait_ge(s["fx_in"], ONE + (at.index("experts") + 1) * 32)
                        pe.wait_ge(s["experts_ready"], ONE + at.batch("experts") + 1)
                    bank_z.take(("fx_lo_ready", f + 1))
                    for j in range(2):
                        last = t.transpose(ps_z[:, j * SLOTS:(j + 1) * SLOTS],
                                           fx[:, 2 * pair + j, :, :].rearrange("p a b -> p (a b)"), ident[:])
                    last.then_inc(s["fx_t_done"], 1)
                    picked[pair] = [pe.value_load(
                        tile_expert[0:1, at.batch("experts") % 4,
                                    bass.ds(at.chunk("experts") * SLICE + 2 * pair + j, 1)],
                        min_val=0, max_val=EXPERTS - 1) for j in range(2)]
                elif name == "hidden":
                    bank_x.take(("hid_ready", f + 1))
                    pe.wait_ge(s["fx_lo_ready"], ONE + f + 1)
                    for j in range(2):
                        for part in (fx_hi, fx_lo):
                            last = t.matmul(ps_x[:, j * 2 * HIDDEN:(j + 1) * 2 * HIDDEN], part[:, j * SLOTS:(j + 1) * SLOTS],
                                            w12[:, bass.ds(picked[pair][j], 1), :].rearrange("p a b -> p (a b)"),
                                            start=(part is fx_hi), stop=(part is fx_lo))
                    last.then_inc(s["h_done"], 1)
                elif name == "turn":
                    bank_z.take(("ht_ready", f + 1))
                    pe.wait_ge(s["hid_ready"], ONE + f + 1)
                    for j in range(2):
                        last = t.transpose(ps_z[:, j * SLOTS:(j + 1) * SLOTS], hid[:, j, :], ident[:])
                    last.then_inc(s["ht_done"], 1)
                else:
                    bank_x.take(("fy_ready", f + 1))
                    pe.wait_ge(s["ht_ready"], ONE + f + 1)
                    for j in range(2):
                        last = t.matmul(ps_x[:, j * CHANNELS:(j + 1) * CHANNELS], hidT[:, j * SLOTS:(j + 1) * SLOTS],
                                        w3s[:, bass.ds(picked[pair][j], 1), :].rearrange("p a b -> p (a b)"),
                                        start=True, stop=True)
                    last.then_inc(s["y_done"], 1)

            events = {"conv": conv, "tokens": tokens, "turned": turned,
                      "query": lambda at: project(at, 0, "q_f_ready", "q_done"),
                      "key": lambda at: project(at, 1, "k_f_ready", "k_done"),
                      "attended": attended, "turned2": turned2, "gate": gate, "combine": combine, "stats": stats}

            def body(at):
                pre, post, f, k = (at.index(n) for n in ("pre", "post", "experts", "combine"))
                bank_x.readers = [("fy_ready", f * PAIRS)]
                bank_z.readers = [("ht_ready", f * PAIRS), ("xconv_ready", pre)]
                bank_y.readers = [] if at.attends and not (at.static and at.c == 0) else \
                    [("k_f_ready", pre), ("logit_used", post), ("out_ready", k),
                     ("rank_ready", min(max(at.u - (at.static and at.c == 0), 0), BATCHES)),
                     ("gn_var_ready", min(max(at.u + 2, 0), BATCHES))]
                routes = at.static and at.c == 0 and at.active("post")
                done = 0
                for i in range(TILES):
                    if at.attends:
                        scores(at, i)
                        if i:
                            weigh(at, i - 1)
                    if at.ahead:
                        reach = max_reach(i)
                        maxima(at.n + 1, at.next_u, range(done, reach))
                        done = reach
                    for step, stage, name in STEPS:
                        if step == i and name in events and at.active(stage):
                            events[name](at)
                    for step, name, pair in EXPERT_STEPS:
                        if step == i and at.active("experts"):
                            expert(at, name, pair)
                    if routes and i == 11:
                        route_total(at.batch("post"))
                    if routes and i == 12:
                        route_rank(at.batch("post"))
                if at.ahead:
                    bank_y.take()
                    shift(at.n + 1)
                if at.attends:
                    weigh(at, TILES - 1)
                if at.u == -1 and at.static and at.c == CHUNKS - 1:
                    maxima(0, 0, range(TILES))
                    bank_y.take()
                    shift(0)

            iterations(pe, body)


def max_reach(i):
    return min(TILES, max(0, -(-(i - MAX_FROM + 1) * TILES // (MAX_TO - MAX_FROM))))


STEPS_POOL = sorted(STEPS, key=lambda step: {"norm1": 0, "gather": 1, "norm2": 2, "scatter": 3}.get(step[2], 4))


INPUTS = ["x", "L0_conv_weight", "L1_attn_Wq", "L1_attn_bq", "L1_attn_Wk", "L1_attn_bk", "L1_attn_Wv", "L1_attn_bv",
          "L1_ffn_gate_w", "L1_ffn_gate_b", "L1_ffn_w1", "L1_ffn_w2", "L1_ffn_w3"]


def kernel(**inputs):
    import numpy as np
    import concourse.bacc as bacc
    from concourse.bass_utils import run_bass_kernel_spmd

    nc = bacc.Bacc("TRN2", target_bir_lowering=False, num_devices=1)
    arrays, args = {}, []
    for name in INPUTS:
        a = np.ascontiguousarray(inputs[name])
        arrays[f"in_{name}"] = a
        args.append(nc.dram_tensor(f"in_{name}", a.shape, mybir.dt.from_np(a.dtype), kind="ExternalInput").ap())
    args.append(nc.dram_tensor("out_x", (BATCHES, CHANNELS, SIDE, SIDE), f32, kind="ExternalOutput").ap())
    build(nc, *args)
    return run_bass_kernel_spmd(nc, [arrays], core_ids=[0]).results[0]["out_x"]
```

```python
import concourse.bass as bass
from concourse import mybir
from contextlib import ExitStack

f32 = mybir.dt.float32
f32r = mybir.dt.float32r
i32 = mybir.dt.int32
u32 = mybir.dt.uint32
ALU = mybir.AluOpType
ACT = mybir.ActivationFunctionType
AX = mybir.AxisListType

BATCHES, CHANNELS, SIDE = 8, 64, 56
TOKENS = SIDE * SIDE
ROWS = 8
CHUNK = ROWS * SIDE
CHUNKS = TOKENS // CHUNK
ALL = BATCHES * CHUNKS
TILE = 112
PER = CHUNK // TILE
TILES = TOKENS // TILE
PAD = SIDE + 2
TAPS = 9
EXPERTS, HIDDEN, TOP = 16, 128, 2
SLOTS = 128
SORTED_MOST = TOP * TOKENS // SLOTS + EXPERTS - 1
SLICE = -(-SORTED_MOST // CHUNKS)
PAIRS = SLICE // 2
SORTED_TILES = SLICE * CHUNKS
DIGIT = EXPERTS.bit_length() - 1
LAST_PAIRS = -(-(SORTED_MOST - SLICE * (CHUNKS - 1)) // 2)
ALL_PAIRS = PAIRS * (CHUNKS - 1) + LAST_PAIRS
FX_PARTS = ((0, 3), (3, PAIRS))
VCOLS = CHANNELS + 1
GN_EPS, LN_EPS = 1e-5, 1e-5
ONE = 1
ZEROS = 16 * CHUNKS

assert SLICE % 2 == 0 and TOKENS % CHUNK == 0 and 0 < LAST_PAIRS <= FX_PARTS[0][1]

LAG = {"pre": -CHUNKS, "post": 1, "scatter": 1 + CHUNKS, "experts": 1 + 2 * CHUNKS, "combine": 1 + 3 * CHUNKS}
STEPS = [(2, "post", "attended"), (2, "pre", "normed"), (3, "post", "residual"), (3, "post", "norm2"),
         (3, "scatter", "rows"), (4, "held", "hold"), (4, "pre", "conv"), (4, "pre", "convolved"), (5, "post", "apply2"),
         (6, "post", "turned2"), (7, "pre", "tokens"), (8, "pre", "norm1"),
         (9, "post", "gate"), (10, "post", "picked"), (11, "post", "gate_exp"), (11, "pre", "apply1"),
         (12, "post", "gates"), (13, "pre", "turned"), (13, "pre", "turned_low"), (14, "pre", "query"),
         (15, "pre", "key"), (19, "combine", "combine"), (21, "combine", "combined"), (23, "stats", "stats"),
         (24, "stats", "mean"), (25, "stats", "deviation"), (26, "stats", "variance"), (27, "stats", "scale")]
EXPERT_STEPS = sorted(
    (at + 5 * g, order, name, g) for g in range(PAIRS) for at, order, name in
    ((1, 1, "fx"), (1, 2, "fx_low"), (3, 3, "hidden"), (3, 4, "gated"), (5, 0, "turn"), (7, 2, "down")))
EXPERT_STEPS_ALONE = sorted(
    (at + 4 * g, order, name, g) for g in range(PAIRS) for at, order, name in
    ((0, 0, "fx"), (0, 1, "fx_low"), (3, 0, "hidden"), (3, 1, "gated"), (5, 0, "turn"), (8, 1, "down")))
NEXT_QUERIES = 0
MAX_FROM, MAX_TO = 2, 27


def wait_apart(engine, sem, value):
    engine.wait_ge(sem, value)
    engine.nop(nofuse=True)


class Link:

    def __init__(self, engine, sem, start):
        self.engine, self.sem, self.start, self.count = engine, sem, start, 0

    def __call__(self, instruction, apart=False):
        instruction.then_inc(self.sem, 1)
        self.count += 1
        (wait_apart if apart else type(self.engine).wait_ge)(self.engine, self.sem, ONE + self.start + self.count)


class At:

    def __init__(self, u, c):
        self.u, self.c, self.static = u, c, isinstance(c, int)
        self.n = CHUNKS * u + c
        self.attends = 0 <= u < BATCHES
        self.ahead = self.attends and not (u == BATCHES - 1 and self.static and c == CHUNKS - 1)
        self.next_u = u + 1 if self.static and c == CHUNKS - 1 else u
        self.next_c = 0 if self.static and c == CHUNKS - 1 else c + 1

    def index(self, stage):
        first = CHUNKS * self.u - LAG[stage] + (self.c if self.static else 1)
        last = first if self.static else first + CHUNKS - 3
        if last < 0:
            return 0
        if first >= ALL:
            return ALL
        return CHUNKS * self.u - LAG[stage] + self.c

    def active(self, stage):
        if stage == "held":
            return self.attends
        if stage == "stats":
            return 0 <= self.u + 2 < BATCHES
        first = CHUNKS * self.u - LAG[stage] + (self.c if self.static else 1)
        return 0 <= first < ALL

    def batch(self, stage):
        return (CHUNKS * self.u - LAG[stage] + (self.c if self.static else 1)) // CHUNKS

    def pair_count(self):
        return LAST_PAIRS if self.static and self.chunk("experts") == CHUNKS - 1 else PAIRS

    def pairs_before(self):
        index = self.index("experts")
        if isinstance(index, int):
            return index // CHUNKS * ALL_PAIRS + index % CHUNKS * PAIRS
        return self.batch("experts") * ALL_PAIRS + self.chunk("experts") * PAIRS

    def chunk(self, stage):
        return self.index(stage) - CHUNKS * self.batch(stage)


def iterations(engine, body):
    for u in range(-2, BATCHES + 4):
        if u == -2:
            body(At(u, CHUNKS - 1))
        elif u < BATCHES + 3:
            body(At(u, 0))
            with engine.Fori(1, CHUNKS - 1) as c:
                body(At(u, c))
            body(At(u, CHUNKS - 1))
        else:
            body(At(u, 0))


def build(nc, x, conv_w, wq, bq, wk, bk, wv, bv, gate_w, gate_b, w1, w2, w3, out):
    def scratch(name, shape):
        return nc.dram_tensor(name, shape, f32, kind="Internal").ap()

    sorted_x = [scratch(f"sorted_x{p}", (2 * ALL_PAIRS * SLOTS, CHANNELS)) for p in range(2)]
    sorted_y = [scratch(f"sorted_y{p}", (2 * ALL_PAIRS * SLOTS, CHANNELS)) for p in range(2)]
    kept = scratch("kept", (ALL, TILE, PER * CHANNELS))
    x_v = x.rearrange("b c h w -> b c (h w)")
    out_v = out.rearrange("b c h w -> b c (h w)")

    ctx = ExitStack()
    with ctx:
        def sb(name, shape, dt=f32):
            return ctx.enter_context(nc.sbuf_tensor(name, shape, dt))

        def pb(name, shape, dt=f32):
            return ctx.enter_context(nc.psum_tensor(name, shape, dt))

        ident = sb("ident", [128, 128])
        pair_mean = sb("pair_mean", [128, 128])
        before = sb("before", [TILE, TILE])
        ones = sb("ones", [TILE, TILE])
        minus_half = sb("minus_half", [128, PER])
        expert_i = sb("expert_i", [TILE, EXPERTS], i32)
        expert_f = sb("expert_f", [TILE, EXPERTS])
        tile_i = sb("tile_i", [TILE, SORTED_TILES], i32)
        tile_f = sb("tile_f", [TILE, SORTED_TILES])
        not_first = sb("not_first", [TILE, EXPERTS * TILES])
        raw_w = sb("raw_w", [128, (TAPS + 3) * CHANNELS])
        wT = sb("wT", [128, TAPS + 2, 128], f32r)
        w_out = sb("w_out", [VCOLS, VCOLS])
        w12 = sb("w12", [128, EXPERTS, 2 * HIDDEN], f32r)
        w3s = sb("w3s", [HIDDEN, EXPERTS, CHANNELS])
        gate_s = sb("gate_s", [CHANNELS, EXPERTS])
        gate_bb = sb("gate_bb", [TILE, EXPERTS])
        bq_raw = sb("bq_raw", [128, 1])
        bq_s = sb("bq_s", [128, 1])
        bk_s = sb("bk_s", [128, 1])

        x_st = sb("x_st", [128, CHUNK])
        gn_stats = sb("gn_stats", [128, CHUNKS, 6])
        gn_mv = sb("gn_mv", [128, 2])
        gn_mean, gn_d, gn_q, gn_e, gn_var, gn_rstd, gn_bias = [
            sb(f"gn_{n}", [128, 1]) for n in ("mean", "d", "q", "e", "var", "rstd", "bias")]
        xh = sb("xh", [128, ROWS + 2, SIDE])
        xg_f = sb("xg_f", [128, ROWS + 2, SIDE])
        xg_hi = sb("xg_hi", [128, ROWS + 2, PAD], f32r)
        xg_lo = sb("xg_lo", [128, ROWS + 2, PAD], f32r)
        x_conv = sb("x_conv", [CHANNELS, CHUNK])

        tok = sb("tok", [TILE, TILES, CHANNELS])
        tok_held = sb("tok_held", [TILE, PER, CHANNELS])
        ln_s = sb("ln_s", [TILE, 4, PER])
        ln2_s = sb("ln2_s", [TILE, 4, PER])
        ln_c = sb("ln_c", [TILE, PER, CHANNELS])
        ln2_c = sb("ln2_c", [TILE, PER, CHANNELS])
        ln_q = sb("ln_q", [TILE, PER, CHANNELS])
        xn = sb("xn", [TILE, PER, 2, CHANNELS])
        xn_hi = sb("xn_hi", [128, CHUNK], f32r)
        xn_lo = sb("xn_lo", [128, CHUNK], f32r)
        qk_f = sb("qk_f", [128, 2, CHUNK])
        qk_hi = sb("qk_hi", [128, CHUNK], f32r)
        q_hl = sb("q_hl", [128, TOKENS], f32r)
        k_a = [sb(f"k_a{p}", [128, TOKENS], f32r) for p in range(2)]
        k_b = [sb(f"k_b{p}", [128, TOKENS], f32r) for p in range(2)]
        v_s = [sb(f"v_s{p}", [TILE, TILES, VCOLS]) for p in range(2)]
        q_a = sb("q_a", [128, 2, CHUNK], f32r)
        q_b = sb("q_b", [128, 2, CHUNK], f32r)
        q_max = sb("q_max", [128, CHUNK], f32r)
        prob = [sb(f"prob{i}", [TILE, CHUNK]) for i in range(4)]
        max_part = sb("max_part", [TILE, PER, CHUNKS])
        max_neg = sb("max_neg", [TILE, PER])
        z_s = sb("z_s", [VCOLS, CHUNK])
        row_inv = sb("row_inv", [TILE, PER])
        t_now = sb("t_now", [TILE, PER, CHANNELS])

        xn2 = sb("xn2", [TILE, TILES, CHANNELS])
        xn2_now = sb("xn2_now", [TILE, PER, CHANNELS])
        xn2T = sb("xn2T", [CHANNELS, CHUNK])
        logit = sb("logit", [TILE, PER, EXPERTS])
        top8 = sb("top8", [TILE, PER, 8])
        top8_i = sb("top8_i", [TILE, PER, 8], u32)
        top_f = sb("top_f", [TILE, PER, TOP])
        pick1 = sb("pick1", [TILE, EXPERTS, TILES])
        pick2 = sb("pick2", [TILE, EXPERTS, TILES])
        gates = sb("gates", [TILE, 4, 2, TILES])
        gate_d = sb("gate_d", [TILE, PER])
        gate_e = sb("gate_e", [TILE, PER])
        picks = sb("picks", [TILE, EXPERTS, TILES])
        in_tile = sb("in_tile", [TILE, EXPERTS, TILES])
        upto = sb("upto", [TILE, EXPERTS, TILES])
        total_i = sb("total_i", [TILE, EXPERTS], i32)
        padded = sb("padded", [TILE, EXPERTS])
        run_end = sb("run_end", [TILE, EXPERTS])
        run_start = sb("run_start", [TILE, EXPERTS])
        tile_expert_f = sb("tile_expert_f", [TILE, SORTED_TILES])
        digit = sb("digit", [TILE, SLICE])
        digits = sb("digits", [TILE, CHUNKS, SLICE])
        code_f = sb("code_f", [TILE, CHUNKS, 2])
        codes = sb("codes", [TILE, 4, CHUNKS, 2], i32)
        slot_f = sb("slot_f", [TILE, TOP, TILES])
        slot = sb("slot", [TILE, 4, TOP, TILES], u32)
        row_now = sb("row_now", [TILE, PER, CHANNELS])
        slot_to = sb("slot_to", [TILE, TOP, PER], u32)
        slot_of = sb("slot_of", [TILE, TOP, PER], u32)

        fx = sb("fx", [SLOTS, SLICE, 2, CHANNELS])
        fx_hi = sb("fx_hi", [128, 2 * SLOTS], f32r)
        fx_lo = sb("fx_lo", [128, 2 * SLOTS], f32r)
        th = sb("th", [SLOTS, 2, HIDDEN])
        up = sb("up", [SLOTS, 2, HIDDEN])
        hid = sb("hid", [SLOTS, 2, HIDDEN])
        hidT = sb("hidT", [HIDDEN, 2 * SLOTS])
        fy = sb("fy", [SLOTS, SLICE, CHANNELS])
        spare = (qk_f[:].rearrange("p a c -> p (a c)"), w3s[:].rearrange("p e c -> p (e c)"),
                 fx[:].rearrange("p t a c -> p (t a c)"))
        first_image = [at[:, half * CHUNK:(half + 1) * CHUNK] for at in spare for half in range(2)] + [x_st[:]]
        got1 = sb("got1", [TILE, PER, CHANNELS])
        got2 = sb("got2", [TILE, PER, CHANNELS])
        tc = sb("tc", [TILE, PER, CHANNELS])
        t_out = sb("t_out", [TILE, PER, CHANNELS])
        out_s = sb("out_s", [CHANNELS, CHUNK])

        ps_s = [pb(f"ps_s{i}", [128, 512]) for i in range(2)]
        ps_m = [pb(f"ps_m{i}", [128, 512]) for i in range(2)]
        ps_o = pb("ps_o", [128, 512])
        ps_x = pb("ps_x", [128, 512])
        ps_y = pb("ps_y", [128, 512])
        ps_z = pb("ps_z", [128, 512])

        started = ctx.enter_context(nc.semaphore("started"))
        names = """weights_in w12_in w_twice wt_done wt_ready w_link bq_ready consts pool_chain
            w12_link w12_ready image_in w3_in x_st_in stats_done gn_link gn_mean_ready gn_mean_done gn_dev_ready gn_var_done
            gn_var_ready gn_rstd_ready gn_scale_ready xh_in xg_ready xg_hi_ready xg_lo_ready border_ready
            conv_done xconv_ready tt_done tok_ready ln_link ln_var ln_rstd xn_ready xt_done v_ready xn_hi_ready
            xn_lo_ready q_done k_done q_f_ready k_f_ready qk_link q_ready k_ready
            qa_ready qmax_ready max_done max_red maxneg_ready shiftT_done shift_ready s_done p_ready pv_done
            z_ready outp_done o_link o_used t_out_dma
            ln2_link r_var r_rstd r_xn_ready r_t_done r_t_ready logit_done r_link gates_link logit_used gate_d_ready gate_e_ready
            gate_ready picks_ready total_done total_ready rank_done rank_ready rt_link slots_ready experts_ready
            slot_to_ready row_ready held scattered fx_a_in fx_b_in fx_t_done fx_hi_ready fx_lo_ready h_done th_ready f_link hid_ready ht_done
            ht_ready y_done fy_ready fy_out slot_of_ready gathered tc_in c_link c_ready c_t_done out_ready
            stored""".split()
        s = {n: ctx.enter_context(nc.semaphore(n)) for n in names}

        block = ctx.enter_context(nc.Block())

        def cols(c):
            return bass.ds(c * CHUNK, CHUNK)

        def tiles(c):
            return bass.ds(c * PER, PER)

        def halo(at):
            if at.static and at.c == 0:
                return slice(1, ROWS + 2)
            return slice(0, ROWS + 1 if at.static and at.c == CHUNKS - 1 else ROWS + 2)

        @block.sync
        def _(sp):
            sp.wait_ge(started, 1)
            for half in range(2):
                for c in range(CHUNKS):
                    sp.dma_start(first_image[c][64 * half:64 * half + 64, :], x_v[0, :, c * CHUNK:(c + 1) * CHUNK])\
                        .then_inc(s["image_in"], 16)
            for half in range(2):
                rows = slice(64 * half, 64 * half + 64)
                sp.dma_start(raw_w[rows, 0:TAPS * CHANNELS], conv_w).then_inc(s["weights_in"], 16)
                for m, w in enumerate((wq, wk, wv)):
                    to = (TAPS + m) * CHANNELS
                    sp.dma_start(raw_w[rows, to:to + CHANNELS], w).then_inc(s["weights_in"], 16)
                sp.dma_start(bq_raw[rows, :], bq.rearrange("(c a) -> c a", a=1)).then_inc(s["weights_in"], 16)
                sp.dma_start(bk_s[rows, :], bk.rearrange("(c a) -> c a", a=1)).then_inc(s["weights_in"], 16)
            sp.dma_start(w_out[CHANNELS:VCOLS, 0:CHANNELS], bv.rearrange("(a c) -> a c", a=1)).then_inc(s["weights_in"], 16)
            sp.dma_start(gate_bb[:], gate_b.rearrange("(a c) -> a c", a=1).partition_broadcast(TILE)
                         .rearrange("p a c -> p (a c)")).then_inc(s["weights_in"], 16)
            sp.dma_start(gate_s[:], gate_w).then_inc(s["weights_in"], 16)

            def load_halo(b, c, first, rows, count):
                wait_apart(sp, s["xconv_ready"], ONE + count)
                for half in range(2):
                    sp.dma_start(xh[64 * half:64 * half + 64, rows, :].rearrange("p h w -> p (h w)"),
                                 x_v[b, :, bass.ds(first * SIDE, (rows.stop - rows.start) * SIDE)])\
                        .then_inc(s["xh_in"], 16)

            def load_slice(at, part):
                nxt = At(at.next_u, at.next_c) if at.static else None
                active, b, c, count = (at.active("experts"), at.batch("experts"), at.chunk("experts") + 1, PAIRS) \
                    if nxt is None else \
                    (nxt.active("experts"), nxt.batch("experts"), nxt.chunk("experts"), nxt.pair_count())
                first, last = FX_PARTS[part]
                if active and first < count:
                    if part == 0:
                        wait_apart(sp, s["scattered"], ZEROS + (b + 1) * (16 * TOP * TILES))
                    if at.active("experts"):
                        wait_apart(sp, s["fx_t_done"], ONE + at.pairs_before() + min(last, at.pair_count()))
                    last = min(last, count)
                    for twice in range(2):
                        sp.dma_start(fx[:, 2 * first:2 * last, twice, :],
                                     sorted_x[b % 2][bass.ds((c * SLICE + 2 * first) * SLOTS, 2 * (last - first) * SLOTS)]
                                     .rearrange("(t p) c -> p t c", p=SLOTS)).then_inc((s["fx_a_in"], s["fx_b_in"])[part], 16)

            def store_out(at):
                k = at.index("combine")
                wait_apart(sp, s["out_ready"], ONE + k + 1)
                sp.dma_start(out_v[at.batch("combine"), :, cols(at.chunk("combine"))], out_s[:]).then_inc(s["stored"], 16)

            def body(at, following=None):
                if at.active("stats") and at.u > -2:
                    n = at.n + 2 * CHUNKS
                    wait_apart(sp, s["stats_done"], ONE + n)
                    for half in range(2):
                        sp.dma_start(x_st[64 * half:64 * half + 64, :], x_v[at.u + 2, :, cols(at.c)])\
                            .then_inc(s["x_st_in"], 16)
                if at.active("combine"):
                    k = at.index("combine")
                    wait_apart(sp, s["c_ready"], ONE + k)
                    sp.dma_start(tc[:].rearrange("p a c -> p (a c)"),
                                 kept[bass.ds(k, 1)].rearrange("a p c -> (a p) c")).then_inc(s["tc_in"], 16)
                if at.u == -2:
                    sp.wait_ge(s["stats_done"], ONE + CHUNKS)
                    sp.dma_start(w3s[:], w3.rearrange("e h c -> h e c")).then_inc(s["w3_in"], 16)
                    load_halo(0, 0, 0, slice(1, ROWS + 2), 0)
                if at.u == -1:
                    for pair in [at.c, at.c + 1] if at.static and at.c == CHUNKS - 1 else [at.c]:
                        wait_apart(sp, s["w12_ready"], ONE + pair)
                        for half in range(2):
                            for m, w in enumerate((w1, w2)):
                                sp.dma_start((th, up)[m][64 * half:64 * half + 64],
                                             w[bass.ds(pair * 2, 2)].rearrange("e c h -> c e h")).then_inc(s["w12_in"], 16)
                if at.active("post"):
                    r = at.index("post")
                    wait_apart(sp, s["o_used"], ONE + r + 1)
                    sp.dma_start(kept[bass.ds(r, 1)].rearrange("a p c -> (a p) c"),
                                 t_now[:].rearrange("p a c -> p (a c)")).then_inc(s["t_out_dma"], 16)
                if at.active("pre") and following is not None:
                    b, c, rows = following
                    load_halo(b, c, c * ROWS - 1 if rows.start == 0 else 0, rows, at.index("pre") + 1)
                load_slice(at, 0)
                if at.active("combine") and at.attends:
                    store_out(at)
                load_slice(at, 1)
                if at.active("combine") and not at.attends:
                    store_out(at)
                if at.active("experts"):
                    many = 2 * at.pair_count()
                    wait_apart(sp, s["fy_ready"], ONE + at.pairs_before() + at.pair_count())
                    if at.batch("experts") >= 2:
                        wait_apart(sp, s["gathered"], ZEROS + (at.batch("experts") - 1) * (16 * TOP * TILES))
                    sp.dma_start(sorted_y[at.batch("experts") % 2][bass.ds(at.chunk("experts") * (SLICE * SLOTS), many * SLOTS)]
                                 .rearrange("(t p) c -> p t c", p=SLOTS), fy[:, 0:many, :]).then_inc(s["fy_out"], 16)

            everything = slice(0, ROWS + 2)
            body(At(-2, CHUNKS - 1))
            for u in range(-1, BATCHES + 4):
                if u == BATCHES + 3:
                    body(At(u, 0))
                    break
                body(At(u, 0), (u + 1, 1, everything))
                with sp.Fori(1, CHUNKS - 2) as c:
                    body(At(u, c), (u + 1, c + 1, everything))
                five = At(u, CHUNKS - 2)
                body(five, (u + 1, CHUNKS - 1, slice(0, ROWS + 1)))
                body(At(u, CHUNKS - 1), (u + 2, 0, slice(1, ROWS + 2)) if u + 2 < BATCHES else None)
            sp.wait_ge(s["stored"], ONE + 16 * ALL)

        @block.gpsimd
        def _(pool):
            g = nc.gpsimd
            for n in names:
                if n not in ("scattered", "gathered"):
                    g.sem_inc(s[n], 1)
            g.sem_inc(started, 1)
            pool.wait_ge(started, 1)
            chain = Link(pool, s["pool_chain"], 0)
            chain(g.memset(ident[:], 0.0))
            chain(g.affine_select(out=ident[:], in_=ident[:], compare_op=ALU.not_equal, fill=1.0, base=0,
                                  pattern=[[-1, 128]], channel_multiplier=1))
            chain(g.memset(pair_mean[:], 0.5))
            pm = pair_mean[:].rearrange("p (j k) -> p j k", k=2)
            chain(g.affine_select(out=pm, in_=pm, compare_op=ALU.is_ge, fill=0.0, base=0,
                                  pattern=[[-2, 64], [0, 2]], channel_multiplier=1))
            chain(g.affine_select(out=pm, in_=pm, compare_op=ALU.is_ge, fill=0.0, base=1,
                                  pattern=[[2, 64], [0, 2]], channel_multiplier=-1))
            chain(g.memset(ones[:], 1.0))
            chain(g.affine_select(out=before[:], in_=ones[:], compare_op=ALU.is_gt, fill=0.0, base=0,
                                  pattern=[[1, TILE]], channel_multiplier=-1))
            chain(g.memset(minus_half[:], -0.5))
            for first, last in FX_PARTS:
                for j in range(2 * (last - first)):
                    chain(g.memset(digit[:, 2 * first + j:2 * first + j + 1], float(EXPERTS ** j)))
            chain(g.iota(expert_i[:], pattern=[[1, EXPERTS]], base=0, channel_multiplier=0))
            chain(g.iota(tile_i[:], pattern=[[SLOTS, SORTED_TILES]], base=0, channel_multiplier=0))
            chain(g.tensor_copy(expert_f[:], expert_i[:]))
            chain(g.tensor_copy(tile_f[:], tile_i[:]))
            chain(g.memset(not_first[:], 1.0))
            chain(g.memset(not_first[:].rearrange("p (e t) -> p e t", t=TILES)[:, :, 0:1], 0.0))
            for part in (xg_hi, xg_lo):
                chain(g.memset(part[:].bitcast(f32), 0.0))
            for p in range(2):
                chain(g.memset(v_s[p][:, :, CHANNELS:VCOLS], 1.0))
                chain(g.memset(k_b[p][:].bitcast(f32), 1.0))
            chain(g.memset(w_out[0:CHANNELS, CHANNELS:VCOLS], 0.0))
            chain(g.memset(fy[:], 0.0))
            g.memset(gn_q[:], 0.0).then_inc(s["consts"], 1)
            for p in range(2):
                for c in range(CHUNKS):
                    many = min(SLICE, 2 * ALL_PAIRS - c * SLICE)
                    g.dma_start(sorted_x[p][c * SLICE * SLOTS:(c * SLICE + many) * SLOTS]
                                .rearrange("(t p) c -> p t c", p=SLOTS), fy[:, 0:many, :]).then_inc((s["scattered"], s["gathered"])[p], 16)
            pool.wait_ge(s["scattered"], ZEROS + 0)
            pool.wait_ge(s["gathered"], ZEROS + 0)

            def scatter(at):
                m, b = at.index("scatter"), at.batch("scatter")
                wait_apart(pool, s["slots_ready"], ONE + b + 1)
                wait_apart(pool, s["scattered"], ZEROS + m * (16 * TOP * PER))
                if b >= 2:
                    wait_apart(pool, s["fx_a_in"], ONE + (b - 1) * CHUNKS * 32)
                    wait_apart(pool, s["fx_b_in"], ONE + (b - 1) * (CHUNKS - 1) * 32)
                g.tensor_copy(slot_to[:], slot[:, b % 4, :, tiles(at.chunk("scatter"))]).then_inc(s["slot_to_ready"], 1)
                wait_apart(pool, s["slot_to_ready"], ONE + m + 1)
                wait_apart(pool, s["row_ready"], ONE + m + 1)
                for j in range(PER):
                    for k in range(TOP):
                        g.indirect_dma_start(
                            out=sorted_x[b % 2], out_offset=bass.IndirectOffsetOnAxis(ap=slot_to[:, k, j:j + 1], axis=0),
                            in_=row_now[:, j, :], in_offset=None).then_inc(s["scattered"], 16)

            def gather(at):
                k, b = at.index("combine"), at.batch("combine")
                wait_apart(pool, s["fy_out"], ONE + (b + 1) * CHUNKS * 16)
                wait_apart(pool, s["c_ready"], ONE + k)
                g.tensor_copy(slot_of[:], slot[:, b % 4, :, tiles(at.chunk("combine"))]).then_inc(s["slot_of_ready"], 1)
                wait_apart(pool, s["slot_of_ready"], ONE + k + 1)
                for j in range(PER):
                    for m, got in enumerate((got1, got2)):
                        g.indirect_dma_start(
                            out=got[:, j, :], out_offset=None, in_=sorted_y[b % 2],
                            in_offset=bass.IndirectOffsetOnAxis(ap=slot_of[:, m, j:j + 1], axis=0)).then_inc(s["gathered"], 16)

            def norm1(at):
                wait_apart(pool, s["ln_var"], ONE + at.index("pre") + 1)
                g.tensor_tensor(ln_s[:, 3, :], ln_s[:, 2, :], minus_half[0:TILE, :], ALU.pow).then_inc(s["ln_rstd"], 1)

            def norm2(at):
                wait_apart(pool, s["r_var"], ONE + at.index("post") + 1)
                g.tensor_tensor(ln2_s[:, 3, :], ln2_s[:, 2, :], minus_half[0:TILE, :], ALU.pow).then_inc(s["r_rstd"], 1)

            def body(at):
                for stage, name in (("post", norm2), ("pre", norm1), ("combine", gather), ("scatter", scatter)):
                    if at.active(stage):
                        name(at)
                if at.active("stats") and at.static and at.c == CHUNKS - 1:
                    wait_apart(pool, s["gn_var_ready"], ONE + at.u + 3)
                    g.tensor_tensor(gn_rstd[:], gn_var[:], minus_half[:, 0:1], ALU.pow).then_inc(s["gn_rstd_ready"], 1)

            iterations(pool, body)

        @block.scalar
        def _(act):
            a = nc.scalar
            act.wait_ge(started, 1)
            act.wait_ge(s["weights_in"], ONE + 16 * 15)
            a.mul(bq_s[:], bq_raw[:], 0.125).then_inc(s["bq_ready"], 1)
            act.wait_ge(s["bq_ready"], ONE + 1)

            def normed(at):
                n, rows = at.index("pre"), halo(at)
                act.wait_ge(s["gn_scale_ready"], ONE + at.batch("pre") + 1)
                act.wait_ge(s["xh_in"], ONE + (n + 1) * 32)
                act.wait_ge(s["xg_lo_ready"], ONE + n)
                a.activation(xg_f[:, rows, :], xh[:, rows, :], ACT.Identity, bias=gn_bias[:], scale=gn_rstd[:])\
                    .then_inc(s["xg_ready"], 1)

            def hold(at):
                wait_apart(act, s["o_used"], ONE + at.n)
                a.activation(tok_held[:], tok[:, tiles(at.c), :], ACT.Copy).then_inc(s["held"], 1)

            def tokens(at):
                n = at.index("pre")
                if at.attends:
                    act.wait_ge(s["held"], ONE + at.n + 1)
                wait_apart(act, s["tt_done"], ONE + n + 1)
                a.activation(tok[:, tiles(at.c), :],
                             ps_y[0:TILE, 0:PER * CHANNELS].rearrange("p (t c) -> p t c", c=CHANNELS), ACT.Copy)\
                    .then_inc(s["tok_ready"], 1)

            def turned(at):
                n = at.index("pre")
                act.wait_ge(s["xt_done"], ONE + n + 1)
                act.wait_ge(s["k_done"], ONE + n)
                a.activation(xn_hi[:], ps_y[:, 0:CHUNK], ACT.Copy).then_inc(s["xn_hi_ready"], 1)
                a.activation(v_s[at.batch("pre") % 2][:, tiles(at.c), 0:CHANNELS], xn[:, :, 0, :], ACT.Copy)\
                    .then_inc(s["v_ready"], 1)

            def query(at):
                n = at.index("pre")
                act.wait_ge(s["q_done"], ONE + n + 1)
                act.wait_ge(s["q_ready"], ONE + n)
                a.activation(qk_f[:, 0, :], ps_y[:, 0:CHUNK], ACT.Identity, bias=bq_s[:], scale=0.125)\
                    .then_inc(s["q_f_ready"], 1)

            def key(at):
                n = at.index("pre")
                act.wait_ge(s["k_done"], ONE + n + 1)
                act.wait_ge(s["k_ready"], ONE + n)
                a.activation(qk_f[:, 1, :], ps_y[:, 0:CHUNK], ACT.Identity, bias=bk_s[:], scale=1.0)\
                    .then_inc(s["k_f_ready"], 1)

            def turned2(at):
                r = at.index("post")
                act.wait_ge(s["r_t_done"], ONE + r + 1)
                act.wait_ge(s["logit_done"], ONE + r)
                a.activation(xn2T[:], ps_y[0:CHANNELS, 0:CHUNK], ACT.Copy).then_inc(s["r_t_ready"], 1)

            def gate_exp(at):
                r = at.index("post")
                act.wait_ge(s["gate_d_ready"], ONE + r + 1)
                act.wait_ge(s["gate_ready"], ONE + r)
                a.activation(gate_e[:], gate_d[:], ACT.Exp).then_inc(s["gate_e_ready"], 1)

            def combined(at):
                k = at.index("combine")
                act.wait_ge(s["c_t_done"], ONE + k + 1)
                act.wait_ge(s["stored"], ONE + k * 16)
                a.activation(out_s[:], ps_y[0:CHANNELS, 0:CHUNK], ACT.Copy).then_inc(s["out_ready"], 1)

            def expert(at, name, pair):
                f = at.pairs_before() + pair
                if name == "fx":
                    act.wait_ge(s["fx_t_done"], ONE + f + 1)
                    act.wait_ge(s["h_done"], ONE + f)
                    a.activation(fx_hi[:], ps_z[:, 0:2 * SLOTS], ACT.Copy).then_inc(s["fx_hi_ready"], 1)
                elif name == "hidden":
                    act.wait_ge(s["h_done"], ONE + f + 1)
                    act.wait_ge(s["hid_ready"], ONE + f)
                    a.activation(th[:], ps_x[:].rearrange("p (t m h) -> p t m h", t=2, m=2)[:, :, 0, :],
                                 ACT.Tanh, scale=0.5).then_inc(s["th_ready"], 1)
                elif name == "turn":
                    act.wait_ge(s["ht_done"], ONE + f + 1)
                    act.wait_ge(s["y_done"], ONE + f)
                    a.activation(hidT[:], (ps_z if at.attends else ps_m[0])[:, 0:2 * SLOTS], ACT.Copy).then_inc(s["ht_ready"], 1)
                elif name == "down":
                    act.wait_ge(s["y_done"], ONE + f + 1)
                    if pair == 0:
                        act.wait_ge(s["fy_out"], ONE + at.index("experts") * 16)
                    a.activation(fy[:, 2 * pair:2 * pair + 2, :],
                                 (ps_x if at.attends else ps_m[1])[:, 0:2 * CHANNELS].rearrange("p (t c) -> p t c", c=CHANNELS),
                                 ACT.Copy, scale=0.5).then_inc(s["fy_ready"], 1)

            events = {"normed": normed, "hold": hold, "tokens": tokens, "turned": turned, "query": query, "key": key,
                      "turned2": turned2, "gate_exp": gate_exp, "combined": combined}

            def next_queries(n):
                act.wait_ge(s["qa_ready"], ONE + n + 1)
                wait_apart(act, s["max_done"], ONE + n * TILES)
                a.activation(q_max[:], q_a[:, bass.ds(n % 2, 1), :].rearrange("p a c -> p (a c)").bitcast(f32), ACT.Copy)\
                    .then_inc(s["qmax_ready"], 1)

            def next_shift(n):
                wait_apart(act, s["shiftT_done"], ONE + n + 1)
                a.activation(q_b[64:65, bass.ds(n % 2, 1), :].rearrange("p a c -> p (a c)"), ps_y[64:65, 0:CHUNK], ACT.Copy)\
                    .then_inc(s["shift_ready"], 1)

            def body(at):
                for i in range(TILES):
                    if at.attends:
                        act.wait_ge(s["s_done"], ONE + at.n * TILES + (i + 1))
                        a.activation(prob[i % 4][:], ps_s[i % 2][0:TILE, 0:CHUNK], ACT.Exp).then_inc(s["p_ready"], 1)
                    if i == 0 and at.active("post"):
                        act.wait_ge(s["pv_done"], ONE + at.index("post") * TILES + TILES)
                        act.wait_ge(s["outp_done"], ONE + at.index("post"))
                        a.activation(z_s[:], ps_o[0:VCOLS, 0:CHUNK], ACT.Copy).then_inc(s["z_ready"], 1)
                    for step, stage, name in STEPS:
                        if step == i and name in events and at.active(stage):
                            events[name](at)
                    for step, _, name, pair in (EXPERT_STEPS if at.attends else EXPERT_STEPS_ALONE):
                        if step == i and at.active("experts") and pair < at.pair_count():
                            expert(at, name, pair)
                    if i == NEXT_QUERIES + 1 and at.ahead:
                        next_queries(at.n + 1)
                    if i == TILES - 1 and at.ahead:
                        next_shift(at.n + 1)
                if at.u == -1 and at.static and at.c == CHUNKS - 1:
                    next_queries(0)
                    next_shift(0)

            iterations(act, body)

        @block.vector
        def _(dve):
            v = nc.vector
            dve.wait_ge(started, 1)
            dve.wait_ge(s["weights_in"], ONE + 16 * 15)
            dve.wait_ge(s["consts"], ONE + 1)
            taps = raw_w[:, 0:TAPS * CHANNELS].rearrange("p (c k) -> p k c", k=TAPS)
            twice = xg_f[:].rearrange("p h w -> p (h w)")[:, 0:512]
            hi = k_a[0][:, 0:512]
            for g in range(3):
                for m in range(4 * g, 4 * g + 4):
                    w = taps[:, m, :] if m < TAPS else raw_w[:, m * CHANNELS:(m + 1) * CHANNELS]
                    last = v.tensor_copy(twice[:, m % 4 * 128:m % 4 * 128 + 128].rearrange("p (a b) -> p a b", a=2),
                                         w.unsqueeze(1).to_broadcast([128, 2, CHANNELS]))
                last.then_inc(s["w_twice"], 1)
                dve.wait_ge(s["wt_done"], ONE + g + 1)
                many = 4 if g < 2 else 3
                to = wT[:, 4 * g:4 * g + many, :].rearrange("p a b -> p (a b)")
                v.tensor_copy(to[0:64, :], ps_x[0:64, 0:128 * many])
                v.tensor_copy(hi[64:128, 0:128 * many], ps_x[64:128, 0:128 * many]).then_inc(s["w_link"], 1)
                dve.wait_ge(s["w_link"], ONE + g + 1)
                if g == 2:
                    v.tensor_copy(w_out[0:CHANNELS, 0:CHANNELS], ps_x[0:64, 384:448])
                    v.memset(w_out[CHANNELS:VCOLS, CHANNELS:VCOLS], 1.0)
                v.tensor_tensor(to[64:128, :], ps_x[64:128, 0:128 * many], hi[64:128, 0:128 * many].bitcast(f32),
                                ALU.subtract).then_inc(s["wt_ready"], 1)
                dve.wait_ge(s["wt_ready"], ONE + g + 1)

            def expert_weights(pair, keys):
                dve.wait_ge(s["w12_in"], ONE + (pair + 1) * 4 * 16)
                dve.wait_ge(s["k_ready"], ONE + keys)
                for m, raw in enumerate((th, up)):
                    to = w12[:, bass.ds(pair * 2, 2), m * HIDDEN:(m + 1) * HIDDEN]
                    hi = qk_hi[:, 0:2 * HIDDEN].rearrange("p (e h) -> p e h", h=HIDDEN)
                    v.tensor_copy(to[0:64], raw[0:64])
                    v.tensor_copy(hi[64:128], raw[64:128]).then_inc(s["w12_link"], 1)
                    dve.wait_ge(s["w12_link"], ONE + pair * 3 + 2 * m + 1)
                    last = v.tensor_tensor(to[64:128], raw[64:128], hi[64:128].bitcast(f32), ALU.subtract)
                    if m == 0:
                        last.then_inc(s["w12_link"], 1)
                        dve.wait_ge(s["w12_link"], ONE + pair * 3 + 2)
                last.then_inc(s["w12_ready"], 1)
                dve.wait_ge(s["w12_ready"], ONE + pair + 1)

            def layer_norm(link, source, var_sem, ln_c, ln_s):
                link(v.tensor_reduce(ln_s[:, 0, :], source, AX.X, ALU.add))
                link(v.tensor_scalar(ln_s[:, 1, :], ln_s[:, 0, :], 1.0 / CHANNELS, None, ALU.mult))
                link(v.tensor_tensor(ln_c[:], source, ln_s[:, 1, :].unsqueeze(2).to_broadcast([TILE, PER, CHANNELS]),
                                     ALU.subtract))
                link(v.tensor_tensor(ln_q[:], ln_c[:], ln_c[:], ALU.mult))
                link(v.tensor_reduce(ln_s[:, 1, :], ln_q[:], AX.X, ALU.add))
                v.tensor_scalar(ln_s[:, 2, :], ln_s[:, 1, :], 1.0 / CHANNELS, LN_EPS, ALU.mult, ALU.add)\
                    .then_inc(s[var_sem], 1)

            def stats(at):
                n = at.n + 2 * CHUNKS
                if at.u == -2:
                    dve.wait_ge(s["image_in"], ONE + CHUNKS * 32)
                    for c in range(CHUNKS):
                        v.bn_stats(gn_stats[:, c, :], first_image[c]).then_inc(s["stats_done"], 1)
                else:
                    dve.wait_ge(s["x_st_in"], ONE + (n - CHUNKS + 1) * 32)
                    v.bn_stats(gn_stats[:, bass.ds(at.c, 1), :].rearrange("p a b -> p (a b)"), x_st[:]).then_inc(s["stats_done"], 1)
                if not (at.static and at.c == CHUNKS - 1):
                    return
                b = at.u + 2
                wait_apart(dve, s["stats_done"], ONE + (b + 1) * CHUNKS)
                v.bn_aggr(gn_mv[:], gn_stats[:].rearrange("p a b -> p (a b)")).then_inc(s["gn_mean_ready"], 1)

            def last_of_image(event):
                return lambda at: event(at.u + 2) if at.static and at.c == CHUNKS - 1 else None

            def deviation(b):
                link = Link(dve, s["gn_link"], b * 4)
                dve.wait_ge(s["gn_mean_done"], ONE + b + 1)
                link(v.tensor_copy(gn_mean[:], ps_y[:, 0:1]))
                link(v.tensor_tensor(gn_d[:], gn_mv[:, 0:1], gn_mean[:], ALU.subtract))
                link(v.tensor_tensor(gn_q[:], gn_d[:], gn_d[:], ALU.mult))
                v.tensor_tensor(gn_e[:], gn_mv[:, 1:2], gn_q[:], ALU.add).then_inc(s["gn_dev_ready"], 1)

            def scale(b):
                link = Link(dve, s["gn_link"], b * 4 + 3)
                dve.wait_ge(s["gn_var_done"], ONE + b + 1)
                v.tensor_scalar(gn_var[:], ps_y[:, 1:2], GN_EPS, None, ALU.add).then_inc(s["gn_var_ready"], 1)
                dve.wait_ge(s["gn_rstd_ready"], ONE + b + 1)
                link(v.tensor_tensor(gn_q[:], gn_mean[:], gn_rstd[:], ALU.mult))
                v.tensor_scalar(gn_bias[:], gn_q[:], -1.0, None, ALU.mult).then_inc(s["gn_scale_ready"], 1)

            def normed(at):
                n, rows = at.index("pre"), halo(at)
                dve.wait_ge(s["xg_ready"], ONE + n + 1)
                dve.wait_ge(s["conv_done"], ONE + n)
                inner = (slice(None), rows, slice(1, 1 + SIDE))
                v.tensor_copy(xg_hi[inner], xg_f[:, rows, :]).then_inc(s["xg_hi_ready"], 1)
                if at.static:
                    edge = 0 if at.c == 0 else ROWS + 1
                    for part in (xg_hi, xg_lo):
                        last = v.memset(part[:, edge:edge + 1, :].bitcast(f32), 0.0)
                    last.then_inc(s["border_ready"], 1)
                dve.wait_ge(s["xg_hi_ready"], ONE + n + 1)
                v.tensor_tensor(xg_lo[inner], xg_f[:, rows, :], xg_hi[inner].bitcast(f32), ALU.subtract)\
                    .then_inc(s["xg_lo_ready"], 1)

            def conv(at):
                n = at.index("pre")
                dve.wait_ge(s["conv_done"], ONE + n + 1)
                dve.wait_ge(s["tt_done"], ONE + n)
                v.tensor_tensor(x_conv[:], ps_z[0:CHANNELS, 0:CHUNK],
                                xh[0:CHANNELS, 1:ROWS + 1, :].rearrange("p h w -> p (h w)"), ALU.add)\
                    .then_inc(s["xconv_ready"], 1)

            def norm1(at):
                n = at.index("pre")
                dve.wait_ge(s["tok_ready"], ONE + n + 1)
                layer_norm(Link(dve, s["ln_link"], n * 5), tok[:, tiles(at.c), :], "ln_var", ln_c, ln_s)

            def apply1(at):
                n = at.index("pre")
                dve.wait_ge(s["ln_rstd"], ONE + n + 1)
                dve.wait_ge(s["xt_done"], ONE + n)
                dve.wait_ge(s["v_ready"], ONE + n)
                v.tensor_tensor(xn[:], ln_c[:].unsqueeze(2).to_broadcast([TILE, PER, 2, CHANNELS]),
                                ln_s[:, 3, :].unsqueeze(2).unsqueeze(3).to_broadcast([TILE, PER, 2, CHANNELS]),
                                ALU.mult).then_inc(s["xn_ready"], 1)

            def turned(at):
                n = at.index("pre")
                dve.wait_ge(s["xn_hi_ready"], ONE + n + 1)
                v.tensor_tensor(xn_lo[:], ps_y[:, 0:CHUNK], xn_hi[:].bitcast(f32), ALU.subtract).then_inc(s["xn_lo_ready"], 1)

            def query(at):
                n, to = at.index("pre"), q_hl
                dve.wait_ge(s["q_f_ready"], ONE + n + 1)
                v.tensor_copy(to[0:64, cols(at.c)], qk_f[0:64, 0, :])
                v.tensor_copy(qk_hi[64:128, :], qk_f[64:128, 0, :]).then_inc(s["qk_link"], 1)
                dve.wait_ge(s["qk_link"], ONE + n * 2 + 1)
                v.tensor_tensor(to[64:128, cols(at.c)], qk_f[64:128, 0, :], qk_hi[64:128, :].bitcast(f32),
                                ALU.subtract).then_inc(s["q_ready"], 1)

            def key(at):
                n, p = at.index("pre"), at.batch("pre") % 2
                dve.wait_ge(s["k_f_ready"], ONE + n + 1)
                dve.wait_ge(s["q_ready"], ONE + n + 1)
                v.tensor_copy(k_a[p][0:64, cols(at.c)], qk_f[0:64, 1, :])
                v.tensor_copy(k_b[p][0:64, cols(at.c)], qk_f[0:64, 1, :])
                v.tensor_copy(qk_hi[64:128, :], qk_f[64:128, 1, :]).then_inc(s["qk_link"], 1)
                dve.wait_ge(s["qk_link"], ONE + n * 2 + 2)
                v.tensor_tensor(k_a[p][64:128, cols(at.c)], qk_f[64:128, 1, :], qk_hi[64:128, :].bitcast(f32),
                                ALU.subtract).then_inc(s["k_ready"], 1)

            def next_queries(n, c):
                dve.wait_ge(s["q_ready"], ONE + n + 1)
                if not isinstance(n, int) or n:
                    dve.wait_ge(s["s_done"], ONE + (n - 1) * TILES)
                here = bass.ds(n % 2, 1)
                flat = lambda ap: ap.rearrange("p a c -> p (a c)")
                v.tensor_copy(flat(q_b[0:64, here, :]), q_hl[64:128, cols(c)].bitcast(f32))
                v.tensor_copy(flat(q_a[0:64, here, :]), q_hl[0:64, cols(c)].bitcast(f32))
                v.tensor_copy(flat(q_a[64:128, here, :]), q_hl[0:64, cols(c)].bitcast(f32)).then_inc(s["qa_ready"], 1)

            def reduces(n, which):
                for m in which:
                    dve.wait_ge(s["max_done"], ONE + n * TILES + (m + 1))
                    v.tensor_reduce(max_part[:, m % PER, m // PER:m // PER + 1],
                                    ps_m[m % 2][0:TILE, 0:CHUNK], AX.X, ALU.max).then_inc(s["max_red"], 1)

            def max_total(n):
                dve.wait_ge(s["max_red"], ONE + (n + 1) * TILES)
                dve.wait_ge(s["shiftT_done"], ONE + n)
                v.tensor_reduce(max_neg[:], max_part[:], AX.X, ALU.max, negate=True).then_inc(s["maxneg_ready"], 1)

            def attended(at):
                r = at.index("post")
                dve.wait_ge(s["outp_done"], ONE + r + 1)
                dve.wait_ge(s["t_out_dma"], ONE + r * 16)
                dve.wait_ge(s["held"], ONE + r + 1)
                o = ps_y[0:TILE, 0:PER * VCOLS].rearrange("p (t c) -> p t c", c=VCOLS)
                v.reciprocal(row_inv[:], o[:, :, CHANNELS]).then_inc(s["o_link"], 1)
                dve.wait_ge(s["o_link"], ONE + r + 1)
                for j in range(PER):
                    last = v.scalar_tensor_tensor(
                        out=t_now[:, j, :], in0=o[:, j, 0:CHANNELS], scalar=row_inv[:, j:j + 1],
                        in1=tok_held[:, j, :],
                        op0=ALU.mult, op1=ALU.add)
                last.then_inc(s["o_used"], 1)

            def rows(at):
                m = at.index("scatter")
                dve.wait_ge(s["scattered"], ZEROS + m * (16 * TOP * PER))
                v.tensor_copy(row_now[:], xn2[:, tiles(at.chunk("scatter")), :]).then_inc(s["row_ready"], 1)

            def norm2(at):
                r = at.index("post")
                dve.wait_ge(s["o_used"], ONE + r + 1)
                layer_norm(Link(dve, s["ln2_link"], r * 5), t_now[:], "r_var", ln2_c, ln2_s)

            def apply2(at):
                r = at.index("post")
                if at.active("scatter"):
                    dve.wait_ge(s["row_ready"], ONE + at.index("scatter") + 1)
                dve.wait_ge(s["r_rstd"], ONE + r + 1)
                for to in (xn2[:, tiles(at.chunk("post")), :], xn2_now[:]):
                    last = v.tensor_tensor(to, ln2_c[:], ln2_s[:, 3, :].unsqueeze(2).to_broadcast([TILE, PER, CHANNELS]),
                                           ALU.mult)
                last.then_inc(s["r_xn_ready"], 1)

            def gate(at):
                r, b, here = at.index("post"), at.batch("post"), tiles(at.chunk("post"))
                dve.wait_ge(s["logit_done"], ONE + r + 1)
                link = Link(dve, s["r_link"], r * 4)
                v.tensor_tensor(logit[:], ps_y[0:TILE, 0:PER * EXPERTS].rearrange("p (t e) -> p t e", e=EXPERTS),
                                gate_bb[:].unsqueeze(1).to_broadcast([TILE, PER, EXPERTS]), ALU.add)\
                    .then_inc(s["logit_used"], 1)
                wait_apart(dve, s["logit_used"], ONE + r + 1)
                for j in range(PER):
                    last = v.max(top8[:, j, :], logit[:, j, :])
                link(last, True)
                for j in range(PER):
                    last = v.max_index(top8_i[:, j, :], top8[:, j, :], logit[:, j, :])
                v.tensor_tensor(gate_d[:], top8[:, :, 1], top8[:, :, 0], ALU.subtract).then_inc(s["gate_d_ready"], 1)
                link(last)
                link(v.tensor_copy(top_f[:], top8_i[:, :, 0:TOP]))
                for m, pick in enumerate((pick1, pick2)):
                    last = v.tensor_tensor(pick[:, :, here].rearrange("p e t -> p t e"),
                                           expert_f[:].unsqueeze(1).to_broadcast([TILE, PER, EXPERTS]),
                                           top_f[:, :, m:m + 1].to_broadcast([TILE, PER, EXPERTS]), ALU.is_equal)
                link(last)

            def gates_of(at):
                r, b, here = at.index("post"), at.batch("post"), tiles(at.chunk("post"))
                link = Link(dve, s["gates_link"], r * 2)
                dve.wait_ge(s["gate_e_ready"], ONE + r + 1)
                link(v.tensor_scalar(gate_d[:], gate_e[:], 1.0, None, ALU.add))
                link(v.reciprocal(gates[:, b % 4, 0, here], gate_d[:]))
                v.tensor_tensor(gates[:, b % 4, 1, here], gate_e[:], gates[:, b % 4, 0, here], ALU.mult)\
                    .then_inc(s["gate_ready"], 1)

            flat3 = lambda t: t[:].rearrange("p e t -> p (e t)")

            def route_pick(b):
                dve.wait_ge(s["gate_ready"], ONE + (b + 1) * CHUNKS)
                v.tensor_tensor(picks[:], pick1[:], pick2[:], ALU.add).then_inc(s["picks_ready"], 1)

            def route_total(b, link):
                dve.wait_ge(s["total_done"], ONE + b + 1)
                v.tensor_copy(flat3(in_tile), ps_y[0:TILE, 0:EXPERTS * TILES]).then_inc(s["total_ready"], 1)
                dve.wait_ge(s["total_ready"], ONE + b + 1)

            def route_rank(b, link):
                link(v.tensor_tensor_scan(flat3(upto), not_first[:], flat3(in_tile), 0.0, ALU.mult, ALU.add))
                link(v.tensor_scalar(total_i[:], upto[:, :, TILES - 1], float(SLOTS - 1), None, ALU.add))
                link(v.tensor_tensor(upto[:], upto[:], in_tile[:], ALU.subtract))
                dve.wait_ge(s["rank_done"], ONE + b + 1)
                v.tensor_tensor(flat3(upto), flat3(upto), ps_y[0:TILE, 0:EXPERTS * TILES], ALU.add).then_inc(s["rank_ready"], 1)
                dve.wait_ge(s["rank_ready"], ONE + b + 1)

            def route_runs(b, link):
                shift = SLOTS.bit_length() - 1
                link(v.tensor_scalar(total_i[:], total_i[:], shift, shift, ALU.arith_shift_right, ALU.arith_shift_left))
                link(v.tensor_copy(padded[:], total_i[:]))
                link(v.tensor_tensor_scan(run_end[:], ones[:, 0:EXPERTS], padded[:], 0.0, ALU.mult, ALU.add))
                link(v.tensor_tensor(run_start[:], run_end[:], padded[:], ALU.subtract))

            def route_start(b, link):
                link(v.tensor_tensor(upto[:], upto[:], run_start[:].unsqueeze(2).to_broadcast([TILE, EXPERTS, TILES]), ALU.add))

            def route_slot(b, link, m):
                link(v.tensor_tensor(picks[:], (pick1, pick2)[m][:], upto[:], ALU.mult))
                link(v.tensor_reduce(slot_f[:, m, :], picks[:].rearrange("p e t -> p t e"), AX.X, ALU.add))

            def route_slots(b, link):
                v.tensor_copy(slot[:, b % 4, :, :], slot_f[:]).then_inc(s["slots_ready"], 1)
                dve.wait_ge(s["slots_ready"], ONE + b + 1)

            def route_experts(b, link, part):
                share = SORTED_TILES // 5
                these = slice(part * share, (part + 1) * share)
                ended = flat3(picks)[:, 0:share * EXPERTS].rearrange("p (j e) -> p j e", e=EXPERTS)
                link(v.tensor_tensor(ended, run_end[:].unsqueeze(1).to_broadcast([TILE, share, EXPERTS]),
                                     tile_f[:, these].unsqueeze(2).to_broadcast([TILE, share, EXPERTS]), ALU.is_le))
                link(v.tensor_reduce(tile_expert_f[:, these], ended, AX.X, ALU.add))
                if part == 4:
                    link(v.tensor_scalar(tile_expert_f[:], tile_expert_f[:], float(EXPERTS - 1), None, ALU.min))
                    link(v.tensor_tensor(digits[:], tile_expert_f[:].rearrange("p (a b) -> p a b", b=SLICE),
                                         digit[:].unsqueeze(1).to_broadcast([TILE, CHUNKS, SLICE]), ALU.mult))
                    for m, (first, last) in enumerate(FX_PARTS):
                        one = v.tensor_reduce(code_f[:, :, m], digits[:, :, 2 * first:2 * last], AX.X, ALU.add)
                    link(one)
                    v.tensor_copy(codes[:, b % 4, :, :], code_f[:]).then_inc(s["experts_ready"], 1)

            ROUTE = {15: route_total, 16: route_rank, 17: route_runs, 18: route_start, 19: lambda b, l: route_slot(b, l, 0),
                     20: lambda b, l: route_slot(b, l, 1), 21: route_slots,
                     **{22 + k: (lambda b, l, k=k: route_experts(b, l, k)) for k in range(5)}}

            def expert(at, name, pair):
                f = at.pairs_before() + pair
                if name == "fx_low":
                    dve.wait_ge(s["fx_hi_ready"], ONE + f + 1)
                    v.tensor_tensor(fx_lo[:], ps_z[:, 0:2 * SLOTS], fx_hi[:].bitcast(f32), ALU.subtract)\
                        .then_inc(s["fx_lo_ready"], 1)
                elif name == "gated":
                    dve.wait_ge(s["th_ready"], ONE + f + 1)
                    both = ps_x[:].rearrange("p (t m h) -> p t m h", t=2, m=2)
                    v.scalar_tensor_tensor(out=up[:], in0=th[:], scalar=1.0, in1=both[:, :, 0, :],
                                           op0=ALU.add, op1=ALU.mult).then_inc(s["f_link"], 1)
                    dve.wait_ge(s["f_link"], ONE + f + 1)
                    dve.wait_ge(s["ht_done"], ONE + f)
                    v.tensor_tensor(hid[:], up[:], both[:, :, 1, :], ALU.mult).then_inc(s["hid_ready"], 1)

            def combine(at):
                k, b = at.index("combine"), at.batch("combine")
                dve.wait_ge(s["gathered"], ZEROS + (k + 1) * (16 * TOP * PER))
                dve.wait_ge(s["tc_in"], ONE + (k + 1) * 16)
                link = Link(dve, s["c_link"], k * 2)
                for m, got in enumerate((got1, got2)):
                    last = v.tensor_tensor(got[:], got[:], gates[:, b % 4, m, tiles(at.chunk("combine"))].unsqueeze(2)
                                           .to_broadcast([TILE, PER, CHANNELS]), ALU.mult)
                link(last)
                link(v.tensor_tensor(got1[:], got1[:], got2[:], ALU.add))
                dve.wait_ge(s["c_t_done"], ONE + k)
                v.tensor_tensor(t_out[:], tc[:], got1[:], ALU.add).then_inc(s["c_ready"], 1)

            events = {"normed": normed, "convolved": conv, "norm1": norm1, "turned_low": turned, "query": query, "key": key,
                      "apply1": apply1, "residual": attended, "rows": rows, "norm2": norm2, "apply2": apply2, "picked": gate,
                      "gates": gates_of, "combine": combine,
                      "stats": stats, "deviation": last_of_image(deviation), "scale": last_of_image(scale)}

            def body(at):
                routes = at.static and at.c == 0 and at.active("post")
                b = at.batch("post")
                done = 0
                link = Link(dve, s["rt_link"], b * 25)
                for i in range(TILES):
                    if at.ahead:
                        reach = max_reach(i)
                        reduces(at.n + 1, range(done, reach))
                        done = reach
                    for step, stage, name in STEPS:
                        if step == i and name in events and at.active(stage):
                            events[name](at)
                    for step, _, name, pair in (EXPERT_STEPS if at.attends else EXPERT_STEPS_ALONE):
                        if step == i and at.active("experts") and pair < at.pair_count():
                            expert(at, name, pair)
                    if i == 3 and at.u == -1:
                        expert_weights(at.c, at.index("pre"))
                    if routes and i == 14:
                        route_pick(b)
                    if routes and i in ROUTE:
                        ROUTE[i](b, link)
                    if i == NEXT_QUERIES and at.ahead:
                        next_queries(at.n + 1, at.next_c)
                    if i == TILES - 1 and at.ahead:
                        max_total(at.n + 1)
                assert not routes or link.count == 25, link.count
                if at.u == -1 and at.static and at.c == CHUNKS - 1:
                    next_queries(0, 0)
                    reduces(0, range(TILES))
                    max_total(0)
                    expert_weights(CHUNKS, CHUNKS)

            iterations(dve, body)

        @block.tensor
        def _(pe):
            t = nc.tensor
            pe.wait_ge(started, 1)
            pe.wait_ge(s["consts"], ONE + 1)
            twice = xg_f[:].rearrange("p h w -> p (h w)")
            for m in range(TAPS + 3):
                if m % 4 == 0:
                    pe.wait_ge(s["w_twice"], ONE + m // 4 + 1)
                    pe.wait_ge(s["wt_ready"], ONE + m // 4)
                last = t.transpose(ps_x[:, 128 * (m % 4):128 * (m % 4) + 128], twice[:, m % 4 * 128:m % 4 * 128 + 128], ident[:])
                if m % 4 == 3:
                    last.then_inc(s["wt_done"], 1)
            pe.wait_ge(s["wt_ready"], ONE + 3)

            def maxima(n, u, which):
                for m in which:
                    if m == 0:
                        pe.wait_ge(s["qmax_ready"], ONE + n + 1)
                    if m >= 2:
                        pe.wait_ge(s["max_red"], ONE + n * TILES + (m - 1))
                    kb, j = m // PER, m % PER
                    if m == 0:
                        pe.wait_ge(s["k_ready"], ONE + (u + 1) * CHUNKS - 1)
                    if m == TILES - PER:
                        pe.wait_ge(s["k_ready"], ONE + (u + 1) * CHUNKS)
                    t.matmul(ps_m[m % 2][0:TILE, 0:CHUNK], q_max[:, j * TILE:(j + 1) * TILE],
                             k_a[u % 2][:, kb * CHUNK:(kb + 1) * CHUNK], start=True, stop=True).then_inc(s["max_done"], 1)

            def shift(n):
                pe.wait_ge(s["maxneg_ready"], ONE + n + 1)
                for j in range(PER):
                    last = t.transpose(ps_y[:, j * TILE:(j + 1) * TILE],
                                       max_neg[:, j:j + 1].to_broadcast([TILE, 128]), ident[0:TILE, 0:TILE])
                last.then_inc(s["shiftT_done"], 1)

            def scores(at, i):
                p = at.u % 2
                if i == 0:
                    pe.wait_ge(s["shift_ready"], ONE + at.n + 1)
                    pe.wait_ge(s["v_ready"], ONE + (at.u + 1) * CHUNKS)
                if i >= 2:
                    pe.wait_ge(s["p_ready"], ONE + at.n * TILES + (i - 1))
                keys, now = slice(i * TILE, (i + 1) * TILE), bass.ds(at.n % 2, 1)
                t.matmul(ps_s[i % 2][0:TILE, 0:CHUNK], k_a[p][:, keys], q_a[:, now, :].rearrange("p a c -> p (a c)"),
                         start=True, stop=False)
                t.matmul(ps_s[i % 2][0:TILE, 0:CHUNK], k_b[p][0:65, keys], q_b[0:65, now, :].rearrange("p a c -> p (a c)"),
                         start=False, stop=True).then_inc(s["s_done"], 1)

            def weigh(at, i):
                if i == 0:
                    pe.wait_ge(s["z_ready"], ONE + at.n)
                pe.wait_ge(s["p_ready"], ONE + at.n * TILES + (i + 1))
                t.matmul(ps_o[0:VCOLS, 0:CHUNK], v_s[at.u % 2][:, i, :], prob[i % 4][:], start=(i == 0),
                         stop=(i == TILES - 1)).then_inc(s["pv_done"], 1)

            class Bank:

                def __init__(self):
                    self.readers = []

                def take(self, *readers):
                    for name, count in self.readers:
                        wait_apart(pe, s[name], ONE + count)
                    self.readers = list(readers)

            bank_x, bank_y, bank_z, bank_turn, bank_down = Bank(), Bank(), Bank(), Bank(), Bank()

            def conv(at):
                n = at.index("pre")
                bank_z.take(("xconv_ready", n + 1))
                pe.wait_ge(s["xg_lo_ready"], ONE + n + 1)
                for k in range(TAPS):
                    for part in (xg_hi, xg_lo):
                        last = t.matmul(ps_z[:, 0:CHUNK], wT[:, k, :], part[:, k // 3:k // 3 + ROWS, k % 3:k % 3 + SIDE],
                                        start=(k == 0 and part is xg_hi), stop=(k == TAPS - 1 and part is xg_lo))
                last.then_inc(s["conv_done"], 1)

            def tokens(at):
                n = at.index("pre")
                bank_y.take(("tok_ready", n + 1))
                wait_apart(pe, s["xconv_ready"], ONE + n + 1)
                for j in range(PER):
                    last = t.transpose(ps_y[0:TILE, j * CHANNELS:(j + 1) * CHANNELS], x_conv[:, j * TILE:(j + 1) * TILE],
                                       ident[0:CHANNELS, 0:CHANNELS])
                last.then_inc(s["tt_done"], 1)

            def turned(at):
                n = at.index("pre")
                bank_y.take(("xn_lo_ready", n + 1))
                pe.wait_ge(s["xn_ready"], ONE + n + 1)
                for j in range(PER):
                    last = t.transpose(ps_y[:, j * TILE:(j + 1) * TILE], xn[:, j, :, :].rearrange("p a b -> p (a b)"),
                                       ident[0:TILE, 0:TILE])
                last.then_inc(s["xt_done"], 1)

            def project(at, m, ready, done):
                bank_y.take((ready, at.index("pre") + 1))
                t.matmul(ps_y[:, 0:CHUNK], wT[:, TAPS + m, :], xn_hi[:], start=True, stop=False)
                t.matmul(ps_y[:, 0:CHUNK], wT[:, TAPS + m, :], xn_lo[:], start=False, stop=True).then_inc(s[done], 1)

            def attended(at):
                r = at.index("post")
                bank_y.take(("o_used", r + 1))
                pe.wait_ge(s["z_ready"], ONE + r + 1)
                for j in range(PER):
                    last = t.matmul(ps_y[0:TILE, j * VCOLS:(j + 1) * VCOLS], z_s[:, j * TILE:(j + 1) * TILE], w_out[:],
                                    start=True, stop=True)
                last.then_inc(s["outp_done"], 1)

            def turned2(at):
                r = at.index("post")
                bank_y.take(("r_t_ready", r + 1))
                wait_apart(pe, s["r_xn_ready"], ONE + r + 1)
                for j in range(PER):
                    last = t.transpose(ps_y[0:CHANNELS, j * TILE:(j + 1) * TILE], xn2_now[:, j, :], ident[0:TILE, 0:TILE])
                last.then_inc(s["r_t_done"], 1)

            def gate(at):
                r = at.index("post")
                bank_y.take(("logit_used", r + 1))
                for j in range(PER):
                    last = t.matmul(ps_y[0:TILE, j * EXPERTS:(j + 1) * EXPERTS], xn2T[:, j * TILE:(j + 1) * TILE],
                                    gate_s[:], start=True, stop=True)
                last.then_inc(s["logit_done"], 1)

            def combined(at):
                k = at.index("combine")
                bank_y.take(("out_ready", k + 1))
                wait_apart(pe, s["c_ready"], ONE + k + 1)
                for j in range(PER):
                    last = t.transpose(ps_y[0:CHANNELS, j * TILE:(j + 1) * TILE], t_out[:, j, :], ident[0:TILE, 0:TILE])
                last.then_inc(s["c_t_done"], 1)

            def mean(at):
                if at.static and at.c == CHUNKS - 1:
                    b = at.u + 2
                    bank_y.take(("gn_var_ready", b + 1))
                    pe.wait_ge(s["gn_mean_ready"], ONE + b + 1)
                    t.matmul(ps_y[:, 0:1], pair_mean[:], gn_mv[:, 0:1], start=True, stop=True).then_inc(s["gn_mean_done"], 1)

            def variance(at):
                if at.static and at.c == CHUNKS - 1:
                    b = at.u + 2
                    pe.wait_ge(s["gn_dev_ready"], ONE + b + 1)
                    t.matmul(ps_y[:, 1:2], pair_mean[:], gn_e[:], start=True, stop=True).then_inc(s["gn_var_done"], 1)

            flat_picks = picks[:].rearrange("p e t -> p (e t)")

            def route_total(b):
                bank_y.take(("total_ready", b + 1))
                pe.wait_ge(s["picks_ready"], ONE + b + 1)
                t.matmul(ps_y[0:TILE, 0:EXPERTS * TILES], ones[:], flat_picks, start=True, stop=True).then_inc(s["total_done"], 1)

            def route_rank(b):
                bank_y.take(("rank_ready", b + 1))
                t.matmul(ps_y[0:TILE, 0:EXPERTS * TILES], before[:], flat_picks, start=True, stop=True).then_inc(s["rank_done"], 1)

            picked = {}

            def expert(at, name, pair):
                f = at.pairs_before() + pair
                if name == "fx":
                    if pair == FX_PARTS[0][0]:
                        pe.wait_ge(s["fx_a_in"], ONE + (at.index("experts") + 1) * 32)
                    if pair == FX_PARTS[1][0]:
                        pe.wait_ge(s["fx_b_in"], ONE + (at.batch("experts") * (CHUNKS - 1) + at.chunk("experts") + 1) * 32)
                    if pair == 0:
                        pe.wait_ge(s["w3_in"], ONE + 16)
                        pe.wait_ge(s["experts_ready"], ONE + at.batch("experts") + 1)
                    bank_z.take(("fx_lo_ready", f + 1))
                    for j in range(2):
                        last = t.transpose(ps_z[:, j * SLOTS:(j + 1) * SLOTS],
                                           fx[:, 2 * pair + j, :, :].rearrange("p a b -> p (a b)"), ident[:])
                    last.then_inc(s["fx_t_done"], 1)
                    for part, (first, last) in enumerate(FX_PARTS):
                        if pair == first:
                            code = pe.value_load(
                                codes[0:1, at.batch("experts") % 4, bass.ds(at.chunk("experts"), 1), part:part + 1]
                                .rearrange("p a b -> p (a b)"), min_val=0, max_val=EXPERTS ** (2 * (last - first)) - 1)
                            for j in range(2 * (last - first)):
                                picked[2 * first + j] = (code >> (j * DIGIT)) & (EXPERTS - 1)
                elif name == "hidden":
                    bank_x.take(("hid_ready", f + 1))
                    pe.wait_ge(s["fx_lo_ready"], ONE + f + 1)
                    for j in range(2):
                        for part in (fx_hi, fx_lo):
                            last = t.matmul(ps_x[:, j * 2 * HIDDEN:(j + 1) * 2 * HIDDEN], part[:, j * SLOTS:(j + 1) * SLOTS],
                                            w12[:, bass.ds(picked[2 * pair + j], 1), :].rearrange("p a b -> p (a b)"),
                                            start=(part is fx_hi), stop=(part is fx_lo))
                    last.then_inc(s["h_done"], 1)
                elif name == "turn":
                    (bank_z if at.attends else bank_turn).take(("ht_ready", f + 1))
                    pe.wait_ge(s["hid_ready"], ONE + f + 1)
                    for j in range(2):
                        last = t.transpose((ps_z if at.attends else ps_m[0])[:, j * SLOTS:(j + 1) * SLOTS], hid[:, j, :],
                                           ident[:])
                    last.then_inc(s["ht_done"], 1)
                elif name == "down":
                    (bank_x if at.attends else bank_down).take(("fy_ready", f + 1))
                    pe.wait_ge(s["ht_ready"], ONE + f + 1)
                    for j in range(2):
                        last = t.matmul((ps_x if at.attends else ps_m[1])[:, j * CHANNELS:(j + 1) * CHANNELS], hidT[:, j * SLOTS:(j + 1) * SLOTS],
                                        w3s[:, bass.ds(picked[2 * pair + j], 1), :].rearrange("p a b -> p (a b)"),
                                        start=True, stop=True)
                    last.then_inc(s["y_done"], 1)

            events = {"conv": conv, "tokens": tokens, "turned": turned,
                      "query": lambda at: project(at, 0, "q_f_ready", "q_done"),
                      "key": lambda at: project(at, 1, "k_f_ready", "k_done"),
                      "attended": attended, "turned2": turned2, "gate": gate, "combined": combined, "mean": mean,
                      "variance": variance}

            def body(at):
                pre, post, k = (at.index(n) for n in ("pre", "post", "combine"))
                bank_x.readers = [("fy_ready", at.pairs_before())]
                bank_z.readers = [("ht_ready", at.pairs_before()), ("xconv_ready", pre)]
                bank_turn.readers = [("ht_ready", at.pairs_before()), ("max_red", ALL * TILES)]
                bank_down.readers = [("fy_ready", at.pairs_before()), ("max_red", ALL * TILES)]
                bank_y.readers = [] if at.attends and not (at.static and at.c == 0) else \
                    [("k_f_ready", pre), ("logit_used", post), ("out_ready", k),
                     ("rank_ready", min(max(at.u - (at.static and at.c == 0), 0), BATCHES)),
                     ("gn_var_ready", min(max(at.u + 2, 0), BATCHES))]
                routes = at.static and at.c == 0 and at.active("post")
                done = 0
                for i in range(TILES):
                    if at.attends:
                        scores(at, i)
                    reach = max_reach(i)
                    if at.ahead:
                        maxima(at.n + 1, at.next_u, range(done, min(done + 1, reach)))
                    if at.attends and i >= 2:
                        weigh(at, i - 2)
                    if at.ahead:
                        maxima(at.n + 1, at.next_u, range(min(done + 1, reach), reach))
                        done = reach
                    for step, stage, name in STEPS:
                        if step == i and name in events and at.active(stage):
                            events[name](at)
                    for step, _, name, pair in (EXPERT_STEPS if at.attends else EXPERT_STEPS_ALONE):
                        if step == i and at.active("experts") and pair < at.pair_count():
                            expert(at, name, pair)
                    if routes and i == 15:
                        route_total(at.batch("post"))
                    if routes and i == 16:
                        route_rank(at.batch("post"))
                if at.attends:
                    weigh(at, TILES - 2)
                if at.ahead:
                    bank_y.take()
                    shift(at.n + 1)
                if at.attends:
                    weigh(at, TILES - 1)
                if at.u == -1 and at.static and at.c == CHUNKS - 1:
                    maxima(0, 0, range(TILES))
                    bank_y.take()
                    shift(0)

            iterations(pe, body)


def max_reach(i):
    return min(TILES, max(0, -(-(i - MAX_FROM + 1) * TILES // (MAX_TO - MAX_FROM))))


INPUTS = ["x", "L0_conv_weight", "L1_attn_Wq", "L1_attn_bq", "L1_attn_Wk", "L1_attn_bk", "L1_attn_Wv", "L1_attn_bv",
          "L1_ffn_gate_w", "L1_ffn_gate_b", "L1_ffn_w1", "L1_ffn_w2", "L1_ffn_w3"]


def kernel(**inputs):
    import numpy as np
    import concourse.bacc as bacc
    from concourse.bass_utils import run_bass_kernel_spmd

    nc = bacc.Bacc("TRN2", target_bir_lowering=False, num_devices=1)
    arrays, args = {}, []
    for name in INPUTS:
        a = np.ascontiguousarray(inputs[name])
        arrays[f"in_{name}"] = a
        args.append(nc.dram_tensor(f"in_{name}", a.shape, mybir.dt.from_np(a.dtype), kind="ExternalInput").ap())
    args.append(nc.dram_tensor("out_x", (BATCHES, CHANNELS, SIDE, SIDE), f32, kind="ExternalOutput").ap())
    build(nc, *args)
    return run_bass_kernel_spmd(nc, [arrays], core_ids=[0]).results[0]["out_x"]
```
